# Optimizing a Trainium2 kernel written in Bass

```python
import numpy as np
import jax
import jax.numpy as jnp

def _softmax(x, axis=-1):
    return jax.nn.softmax(x, axis=axis)

def _gelu(x):
    return jax.nn.gelu(x, approximate=True)

def _silu(x):
    return jax.nn.silu(x)

def _sigmoid(x):
    return jax.nn.sigmoid(x)

def _layernorm(x, axis=-1, eps=1e-05):
    m = jnp.mean(x, axis=axis, keepdims=True)
    v = jnp.var(x, axis=axis, keepdims=True)
    return (x - m) / jnp.sqrt(v + eps)

def _scatter_add(tgt, idx, src, axis=0):
    return tgt.at[idx].add(src)

def _segment_sum(src, seg, n):
    return jax.ops.segment_sum(src, seg, n)
kernel_name = 'mk_perceiver_d1_seqx_r4_8a0a61'

def setup_inputs(seed: int=0):
    np.random.seed(seed)
    _w = jnp.asarray

    def _rec_inputs():
        import jax
        import jax.numpy as jnp
        _rk = jax.random.key(seed)
        x = 7.22e-05 + 1 * jax.random.normal(jax.random.fold_in(_rk, 1), (8, 64, 256), jnp.float32)
        _lenS = 64 - jax.random.randint(jax.random.fold_in(_rk, 7), (8,), 0, max(1, 64 // 4) + 1, jnp.int32)
        _lenS2 = 1024 - jax.random.randint(jax.random.fold_in(_rk, 8), (8,), 0, max(1, 1024 // 4) + 1, jnp.int32)
        _ctx_1024P = jax.random.normal(jax.random.fold_in(_rk, 11), (8, 16, 256), jnp.float32)
        _ctx_1024c = jax.random.dirichlet(jax.random.fold_in(_rk, 511), 0.3 * jnp.ones((16,), jnp.float32), (8, 1024))
        _ctx_1024t = jnp.einsum('bsk,bkd->bsd', _ctx_1024c, _ctx_1024P)
        _ctx_1024t = _ctx_1024t * jax.lax.rsqrt(jnp.mean(jnp.square(_ctx_1024t)) + 1e-12) * 0.953939
        ctx_1024 = 4.13588e-05 + 0.999923 * (_ctx_1024t + 0.3 * jax.random.normal(jax.random.fold_in(_rk, 611), (8, 1024, 256), jnp.float32))
        return (x, ctx_1024)
    x, ctx_1024 = _rec_inputs()

    def _L0_xattn_setup():
        import jax, jax.numpy as jnp
        import numpy as np
        N_HEAD = 16
        key = jax.random.key(seed)
        ks = jax.random.split(key, 5)
        b, l, d = (4, 512, 256)
        dh = d // N_HEAD
        return {'q': jax.random.normal(ks[0], (b, l, d), dtype=jnp.float32), 'kv': jax.random.normal(ks[1], (b, l, d), dtype=jnp.float32), 'Wq': jax.random.normal(ks[2], (d, d), dtype=jnp.float32) * 0.02, 'Wkv': jax.random.normal(ks[3], (2 * dh, d), dtype=jnp.float32) * 0.02, 'Wc': jax.random.normal(ks[4], (d, d), dtype=jnp.float32) * 0.02}
    _L0_xattn_all = _L0_xattn_setup()
    _L0_xattn_in = {k: v for k, v in _L0_xattn_all.items() if k in ('Wq', 'Wkv', 'Wc')}
    del _L0_xattn_all

    def _L0_attn_setup():
        import jax, jax.numpy as jnp
        import numpy as np
        N_HEADS = 16
        HEAD_DIM = 64
        HIDDEN = 256
        key = jax.random.key(seed)
        kx, kq, kk, kv, ko = jax.random.split(key, 5)
        B, S = (1, 1024)
        lim = float(np.sqrt(6.0 / (HIDDEN + N_HEADS * HEAD_DIM)))
        x = jax.random.normal(kx, (B, S, HIDDEN), dtype=jnp.float32)
        wq = jax.random.uniform(kq, (N_HEADS * HEAD_DIM, HIDDEN), jnp.float32, -lim, lim)
        wk = jax.random.uniform(kk, (N_HEADS * HEAD_DIM, HIDDEN), jnp.float32, -lim, lim)
        wv = jax.random.uniform(kv, (N_HEADS * HEAD_DIM, HIDDEN), jnp.float32, -lim, lim)
        wo = jax.random.uniform(ko, (HIDDEN, N_HEADS * HEAD_DIM), jnp.float32, -lim, lim)
        return {'x': x, 'wq': wq, 'wk': wk, 'wv': wv, 'wo': wo}
    _L0_attn_all = _L0_attn_setup()
    _L0_attn_in = {k: v for k, v in _L0_attn_all.items() if k in ('wq', 'wk', 'wv', 'wo')}
    del _L0_attn_all

    def _L0_ffn_setup():
        import jax, jax.numpy as jnp
        import numpy as np
        H = 16
        TOP_K = 2
        LN_EPS = 1e-05
        key = jax.random.key(seed)
        ks = jax.random.split(key, 8)
        B, S, E, NE = (2, 256, 256, 8)
        w = lambda k, shp: jax.random.normal(k, shp, dtype=jnp.float32) * 0.02
        return {'x': jax.random.normal(ks[0], (B, S, E), dtype=jnp.float32), 'rW1': w(ks[1], (E // 2, E)), 'rb1': jnp.zeros((E // 2,), jnp.float32), 'ln_g': jnp.ones((E // 2,), jnp.float32), 'ln_b': jnp.zeros((E // 2,), jnp.float32), 'rW2': w(ks[2], (NE, E // 2)), 'rb2': jnp.zeros((NE,), jnp.float32), 'qW': w(ks[3], (NE, E, E)), 'qb': jnp.zeros((NE, E), jnp.float32), 'kW': w(ks[4], (NE, E, E)), 'kb': jnp.zeros((NE, E), jnp.float32), 'vW': w(ks[5], (NE, E, E)), 'vb': jnp.zeros((NE, E), jnp.float32), 'oW': w(ks[6], (NE, E, E)), 'ob': jnp.zeros((NE, E), jnp.float32)}
    _L0_ffn_all = _L0_ffn_setup()
    _L0_ffn_in = {k: v for k, v in _L0_ffn_all.items() if k in ('rW1', 'rb1', 'ln_g', 'ln_b', 'rW2', 'rb2', 'qW', 'qb', 'kW', 'kb', 'vW', 'vb', 'oW', 'ob')}
    del _L0_ffn_all
    return {'x': x, 'ctx_1024': ctx_1024, 'L0_xattn_Wq': _L0_xattn_in['Wq'], 'L0_xattn_Wkv': _L0_xattn_in['Wkv'], 'L0_xattn_Wc': _L0_xattn_in['Wc'], 'L0_attn_wq': _L0_attn_in['wq'], 'L0_attn_wk': _L0_attn_in['wk'], 'L0_attn_wv': _L0_attn_in['wv'], 'L0_attn_wo': _L0_attn_in['wo'], 'L0_ffn_rW1': _L0_ffn_in['rW1'], 'L0_ffn_rb1': _L0_ffn_in['rb1'], 'L0_ffn_ln_g': _L0_ffn_in['ln_g'], 'L0_ffn_ln_b': _L0_ffn_in['ln_b'], 'L0_ffn_rW2': _L0_ffn_in['rW2'], 'L0_ffn_rb2': _L0_ffn_in['rb2'], 'L0_ffn_qW': _L0_ffn_in['qW'], 'L0_ffn_qb': _L0_ffn_in['qb'], 'L0_ffn_kW': _L0_ffn_in['kW'], 'L0_ffn_kb': _L0_ffn_in['kb'], 'L0_ffn_vW': _L0_ffn_in['vW'], 'L0_ffn_vb': _L0_ffn_in['vb'], 'L0_ffn_oW': _L0_ffn_in['oW'], 'L0_ffn_ob': _L0_ffn_in['ob']}

def reference(x, ctx_1024, L0_xattn_Wq, L0_xattn_Wkv, L0_xattn_Wc, L0_attn_wq, L0_attn_wk, L0_attn_wv, L0_attn_wo, L0_ffn_rW1, L0_ffn_rb1, L0_ffn_ln_g, L0_ffn_ln_b, L0_ffn_rW2, L0_ffn_rb2, L0_ffn_qW, L0_ffn_qb, L0_ffn_kW, L0_ffn_kb, L0_ffn_vW, L0_ffn_vb, L0_ffn_oW, L0_ffn_ob):
    import jax
    import jax.numpy as jnp

    def _L0_xattn_ref(q, kv, Wq, Wkv, Wc):
        import jax, jax.numpy as jnp
        import numpy as np
        N_HEAD = 16
        b, l, d = q.shape
        h = N_HEAD
        dh = d // h
        qp = jnp.einsum('bld,ed->ble', q, Wq)
        scores = jnp.einsum('bld,bmd->blm', qp, kv)
        idx = jnp.argmax(scores, axis=-1)
        mem = jnp.take_along_axis(kv, idx[..., None], axis=1)
        mkv = jnp.einsum('bld,ed->ble', mem, Wkv)
        mk, mv = jnp.split(mkv, 2, axis=-1)
        qh = qp.reshape(b, l, h, dh).transpose(0, 2, 1, 3)
        scale = 1.0 / np.sqrt(dh).astype(np.float32)
        logits = jnp.einsum('bhld,bmd->bhlm', qh, mk) * scale
        attn = jax.nn.softmax(logits, axis=-1)
        out = jnp.einsum('bhlm,bmd->bhld', attn, mv)
        out = out.transpose(0, 2, 1, 3).reshape(b, l, d)
        return jnp.einsum('bld,ed->ble', out, Wc)

    def _L0_attn_ref(x, wq, wk, wv, wo):
        import jax, jax.numpy as jnp
        import numpy as np
        N_HEADS = 16
        HEAD_DIM = 64
        HIDDEN = 256
        B, S, _ = x.shape
        scale = HEAD_DIM ** (-0.5)

        def proj(w):
            return jnp.einsum('bsh,eh->bse', x, w).reshape(B, S, N_HEADS, HEAD_DIM).transpose(0, 2, 1, 3)
        q, k, v = (proj(wq), proj(wk), proj(wv))
        scores = jnp.einsum('bhqd,bhkd->bhqk', q, k) * scale
        causal = jnp.tril(jnp.ones((S, S), dtype=bool))
        scores = jnp.where(causal, scores, -jnp.inf)
        probs = jax.nn.softmax(scores, axis=-1)
        out = jnp.einsum('bhqk,bhkd->bhqd', probs, v)
        out = out.transpose(0, 2, 1, 3).reshape(B, S, N_HEADS * HEAD_DIM)
        return jnp.einsum('bse,he->bsh', out, wo)

    def _L0_ffn_ref(x, rW1, rb1, ln_g, ln_b, rW2, rb2, qW, qb, kW, kb, vW, vb, oW, ob):
        import jax, jax.numpy as jnp
        import numpy as np
        H = 16
        TOP_K = 2
        LN_EPS = 1e-05
        B, S, E = x.shape
        NE = qW.shape[0]
        Dh = E // H
        scale = 1.0 / jnp.sqrt(jnp.asarray(Dh, x.dtype))
        h = x @ rW1.T + rb1
        mu = h.mean(-1, keepdims=True)
        var = ((h - mu) ** 2).mean(-1, keepdims=True)
        h = (h - mu) * jax.lax.rsqrt(var + LN_EPS) * ln_g + ln_b
        h = jax.nn.relu(h)
        logits = h @ rW2.T + rb2
        probs = jax.nn.softmax(logits, axis=-1)
        tp, ti = jax.lax.top_k(probs, TOP_K)
        tp = tp / tp.sum(-1, keepdims=True)
        expert_mask = (jax.nn.one_hot(ti, NE, dtype=probs.dtype) * tp[..., None]).sum(-2)
        gates = jnp.moveaxis(expert_mask, -1, 0)

        def expert_step(acc, params):
            qw, qb_, kw, kb_, vw, vb_, ow, ob_, g = params
            q = (x @ qw.T + qb_).reshape(B, S, H, Dh).transpose(0, 2, 1, 3)
            k = (x @ kw.T + kb_).reshape(B, S, H, Dh).transpose(0, 2, 1, 3)
            v = (x @ vw.T + vb_).reshape(B, S, H, Dh).transpose(0, 2, 1, 3)
            scores = jnp.einsum('bhqd,bhkd->bhqk', q, k) * scale
            p = jax.nn.softmax(scores, axis=-1)
            o = jnp.einsum('bhqk,bhkd->bhqd', p, v)
            o = o.transpose(0, 2, 1, 3).reshape(B, S, E) @ ow.T + ob_
            return (acc + o * g[..., None], None)
        out, _ = jax.lax.scan(expert_step, jnp.zeros_like(x), (qW, qb, kW, kb, vW, vb, oW, ob, gates))
        return out
    x = x + _L0_xattn_ref(_layernorm(x, axis=-1), ctx_1024, L0_xattn_Wq, L0_xattn_Wkv, L0_xattn_Wc)
    x = x + _L0_attn_ref(_layernorm(x, axis=-1), L0_attn_wq, L0_attn_wk, L0_attn_wv, L0_attn_wo)
    x = x + _L0_ffn_ref(_layernorm(x, axis=-1), L0_ffn_rW1, L0_ffn_rb1, L0_ffn_ln_g, L0_ffn_ln_b, L0_ffn_rW2, L0_ffn_rb2, L0_ffn_qW, L0_ffn_qb, L0_ffn_kW, L0_ffn_kb, L0_ffn_vW, L0_ffn_vb, L0_ffn_oW, L0_ffn_ob)
    return x

_drawn_inputs = setup_inputs


def setup_inputs(seed=0):
    import zlib

    import numpy as np

    out = dict(_drawn_inputs(seed))
    spreads = {'L0_ffn_rb1': (0.0, 0.271),
     'L0_ffn_ln_g': (1.0, 0.2),
     'L0_ffn_ln_b': (0.0, 0.373),
     'L0_ffn_rb2': (0.0, 0.1),
     'L0_ffn_qb': (0.0, 0.8),
     'L0_ffn_kb': (0.0, 0.8),
     'L0_ffn_vb': (0.0, 0.361),
     'L0_ffn_ob': (0.0, 0.1)}
    factors = {'L0_ffn_qW': 8.0, 'L0_ffn_kW': 8.0, 'L0_ffn_vW': 4.051}
    for name, (base, spread) in spreads.items():
        noise = np.random.default_rng([zlib.crc32(name.encode()), seed]).standard_normal(out[name].shape)
        drawn = base * np.exp(spread * noise) if base else spread * noise
        out[name] = jnp.asarray(drawn.astype(out[name].dtype))
    for name, factor in factors.items():
        out[name] = (out[name] * factor).astype(out[name].dtype)
    return out
```

```python
from contextlib import ExitStack

import concourse.bass as bass
from concourse import mybir

F32 = mybir.dt.float32
U32 = mybir.dt.uint32
ALU = mybir.AluOpType
ACT = mybir.ActivationFunctionType
AX = mybir.AxisListType

P = 128
EPS = 1e-5
NORM_GROUPS = [(0, 1, 2, 3), (0, 1), (2, 3), (0, 1), (2, 3), (0, 1, 2, 3)]


class Tile:

    def __init__(self, c, i=None, first=0):
        self.c, self.i = c, i
        self.n = first + c if i is None else 8 * i + (first + c)
        self.two = c % 2
        self.t = c % 4
        self.weights = (c // 4) % 2
        self.expert = c // 4 if i is None else 2 * i + c // 4

    def count(self, per_tile, extra=0):
        return self.n * per_tile + extra


def wait(eng, sem, value):
    if isinstance(value, int) and value <= 0:
        return
    eng.wait_ge(sem, value)


def row_of(dram, e):
    return dram[e] if isinstance(e, int) else dram[bass.ds(e, 1)].squeeze(0)


def build(nc, A):
    x_d, out_d = A["x"], A["out"]
    NT, D, H = 4, 256, 16
    B, L, M = A["ctxT"].shape[0], 64, A["ctxT"].shape[3]
    NE = A["w_qkv"].shape[0]
    C = D // P
    HP = H // 2
    CORE0 = NT
    LAST = NT * NE

    ctx = ExitStack()
    with ctx:
        def sb(name, shape, dt=F32):
            return ctx.enter_context(nc.sbuf_tensor(name, shape, dt))

        def sem(name):
            return ctx.enter_context(nc.semaphore(name))

        bank = [ctx.enter_context(nc.psum_tensor(f"bank{i}", [P, 512], F32)) for i in range(6)]
        match_banks = ctx.enter_context(nc.psum_tensor("bank67", [P, 1024], F32))
        bank += [match_banks[:, 0:512], match_banks[:, 512:1024]]

        const = sb("const", [P, A["const"].shape[1]])
        ident = const[:, 0:128]
        head_mask = const[:, 128:136]
        pair_mask = const[:, 136:138]
        causal = const[:, 138:202]
        iota = const[:, 202:210]
        minus_half = const[:, 210:214]
        row_base = sb("row_base", [P, NT], U32)

        xres = sb("xres", [P, NT, D])
        xn = sb("xn", [P, NT, D])
        xnT = sb("xnT", [P, C, NT * P])
        stats = sb("stats", [P, NT, 6])
        moments = sb("moments", [P, NT, 2])
        rstd = sb("rstd", [P, NT])

        big = sb("big", [P, B * C * M])
        ctxT = big[:, :].rearrange("p (b c m) -> p b c m", b=B, c=C)
        q2T = big[:, 0:8 * 512].rearrange("p (h n) -> p h n", h=HP)
        k2blk = big[:, 4096:12288].rearrange("p (h b j k) -> p h b j k", h=HP, b=B, j=2)
        v2 = big[:, 12288:16384].rearrange("p (b h d) -> p b h d", b=B, h=HP)
        w1q = sb("w1q", [P, C, D])
        w1kv = sb("w1kv", [P, C, 32])
        w1kr = sb("w1kr", [P, C, 8, 16])
        w1c = sb("w1c", [P, C, D])
        q1T = sb("q1T", [P, C, NT * P])
        top8 = sb("top8", [P, NT, 8])
        top8i = sb("top8i", [P, NT, 8], U32)
        rows = sb("rows", [P, NT], U32)
        mem = sb("mem", [P, NT, D])
        memT = sb("memT", [P, 2, C, P])

        w2q = sb("w2q", [P, C, 1024])
        w2k = sb("w2k", [P, C, 1024])
        w2v = sb("w2v", [P, C, 1024])
        w2o = sb("w2o", [P, HP, D])
        O2T = sb("O2T", [P, 2, HP, P])

        rw1 = sb("rw1", [P, C, P])
        rw2 = sb("rw2", [P, NE])
        rb1 = sb("rb1", [P, P])
        lng = sb("lng", [P, P])
        lnb = sb("lnb", [P, P])
        rb2 = sb("rb2", [P, NE])
        hid = sb("hid", [P, NT, P])
        hidT = sb("hidT", [P, NT * P])
        logit = sb("logit", [P, NT, NE])
        prob = sb("prob", [P, NT, NE])
        rtmp = sb("rtmp", [P, 4, NT])
        ptop = sb("ptop", [P, NT, 8])
        itop = sb("itop", [P, NT, 8], U32)
        itopf = sb("itopf", [P, NT, 8])
        pick = sb("pick", [P, 2, NT, NE])
        gates = sb("gates", [P, NT, NE])
        gatesT = sb("gatesT", [NE, NT * P])
        ob = sb("ob", [NE, D])

        wqkv = sb("wqkv", [P, 2, 3 * C * D + 2 * C])
        wo = sb("wo", [P, 2, C, D])
        vb = sb("vb", [P, 2, D])

        def w_of(which, par):
            return wqkv[:, par, which * C * D:(which + 1) * C * D].rearrange("p (c n) -> p c n", c=C)

        qkT = sb("qkT", [P, 2, 2 * C, P])
        kblk = sb("kblk", [P, 2, C, 2, 8, L])
        vblk = sb("vblk", [P, 2, 2, HP, 32])
        E = sb("E", [P, 2, H, L])
        PT = sb("PT", [P, 2, HP, P])
        OT = sb("OT", [P, NT, C, P])
        mx = sb("mx", [P, 2, H])
        ssum = sb("ssum", [P, 2, H])
        recip = sb("recip", [P, 2, H])
        rgate = sb("rgate", [P, 2, H])
        final = xn

        ld = {name: sem(f"ld_{name}") for name in (
            "const", "x", "w1", "router", "w2q", "w2k", "w2v", "w2o", "ob")}
        ld_ctx = [sem(f"ld_ctx{b}") for b in range(B)]
        ld_mem = [sem(f"ld_mem{t}") for t in range(NT)]
        ld_wqkv = [sem(f"ld_wqkv{p}") for p in range(2)]
        ld_wo = [sem(f"ld_wo{p}") for p in range(2)]
        ld_vb = [sem(f"ld_vb{p}") for p in range(2)]
        stored = sem("stored")

        vblk_zero, w1kr_ready = sem("vblk_zero"), sem("w1kr_ready")
        ln_stat, ln_mom, ln_eps, ln_rstd = sem("ln_stat"), sem("ln_mom"), sem("ln_eps"), sem("ln_rstd")
        ln_done = sem("ln_done")
        xT_made, xT_copied = sem("xT_made"), sem("xT_copied")
        x_added = sem("x_added")
        q1_made, q1_copied = sem("q1_made"), sem("q1_copied")
        match_made, match_max, match_read = sem("match_made"), sem("match_max"), sem("match_read")
        rows_ready = sem("rows_ready")
        memT_made, memT_copied = sem("memT_made"), sem("memT_copied")
        kv1_made, k1_copied, v1_copied = sem("kv1_made"), sem("k1_copied"), sem("v1_copied")
        qk_made, qk_copied = sem("qk_made"), sem("qk_copied")
        kblk_ready = sem("kblk_ready")
        v_made, v_copied = sem("v_made"), sem("v_copied")
        s_made = sem("s_made")
        max_done = sem("max_done")
        sub_done = sem("sub_done")
        exp_done = sem("exp_done")
        sum_done = sem("sum_done")
        recip_done, r_ready = sem("recip_done"), sem("r_ready")
        p_ready = sem("p_ready")
        pT_made, pT_copied = sem("pT_made"), sem("pT_copied")
        o_made, o_copied = sem("o_made"), sem("o_copied")
        y_made = sem("y_made")
        p2_made, p2_act, p2_dve = sem("p2_made"), sem("p2_act"), sem("p2_dve")
        s2_made, s2_masked, s2_max, s2_sub, s2_exp, s2_sum, s2_recip, s2_p = (
            sem(f"s2_{n}") for n in ("made", "masked", "max", "sub", "exp", "sum", "recip", "p"))
        pT2_made, pT2_copied = sem("pT2_made"), sem("pT2_copied")
        o2_made, o2_act, o2_dve = sem("o2_made"), sem("o2_act"), sem("o2_dve")
        y2_made = sem("y2_made")
        h_made, hT_made, hT_copied, l_made = sem("h_made"), sem("hT_made"), sem("hT_copied"), sem("l_made")
        r_chain, r_exp_in, r_exp = sem("r_chain"), sem("r_exp_in"), sem("r_exp")
        h_ready, hid_normed = sem("h_ready"), sem("hid_normed")
        gates_ready, gT_made, gT_copied = sem("gates_ready"), sem("gT_made"), sem("gT_copied")
        y_all = sem("y_all")
        final_ready = sem("final_ready")

        block = ctx.enter_context(nc.Block())

        @block.sync
        def _(sp):
            sp.dma_start(xres[:, :, :], x_d.rearrange("(t p) d -> p t d", p=P)).then_inc(ld["x"], 16)
            sp.dma_start(const[:, :], A["const"]).then_inc(ld["const"], 16)
            sp.dma_start(row_base[:, :], A["row_base"]).then_inc(ld["const"], 16)
            sp.dma_start(w1q[:, :, :], A["w1q"]).then_inc(ld["w1"], 16)
            for b in range(B):
                sp.dma_start(ctxT[:, b], A["ctxT"][b]).then_inc(ld_ctx[b], 16)
                if b == 0:
                    sp.dma_start(w1kv[:, :, :], A["w1kv"]).then_inc(ld["w1"], 16)
                    sp.dma_start(w1c[:, :, :], A["w1c"]).then_inc(ld["w1"], 16)
            for name, dst in (("w2q", w2q), ("w2k", w2k), ("w2v", w2v), ("w2o", w2o)):
                sp.dma_start(dst[:, :, :], A[name]).then_inc(ld[name], 16)
            sp.dma_start(rw1[:, :, :], A["rw1"]).then_inc(ld["router"], 16)
            sp.dma_start(rw2[:, :], A["rw2"]).then_inc(ld["router"], 16)
            for dst, name in ((rb1, "rb1"), (lng, "ln_g"), (lnb, "ln_b"), (rb2, "rb2")):
                sp.dma_start(dst[:, :], A[name].partition_broadcast(P)).then_inc(ld["router"], 16)
            sp.dma_start(ob[:, :], A["ob"]).then_inc(ld["ob"], 16)

            def load_expert(e, par, before):
                wait(sp, qk_made, 4 * before)
                wait(sp, v_made, 4 * before)
                sp.dma_start(wqkv[:, par, :], row_of(A["w_qkv"], e)).then_inc(ld_wqkv[par], 16)
                wait(sp, v_copied, 4 * before)
                sp.dma_start(vb[:, par, :], row_of(A["vb"], e).unsqueeze(0).partition_broadcast(P)).then_inc(ld_vb[par], 16)
                if isinstance(before, int) and before <= 0:
                    pass
                else:
                    sp.wait_ge(y_made, 4 * before + CORE0)
                sp.dma_start(wo[:, par, :, :], row_of(A["w_o"], e)).then_inc(ld_wo[par], 16)

            load_expert(0, 0, 0)
            load_expert(1, 1, 0)
            with sp.Fori(1, NE // 2) as i:
                for par in range(2):
                    load_expert(2 * i + par, par, 2 * i + (par - 1))
            for t in range(NT):
                sp.wait_ge(final_ready, t + 1)
                sp.dma_start(out_d.rearrange("(t p) d -> t p d", p=P)[t], final[:, t, :]).then_inc(stored, 16)
            sp.wait_ge(stored, 16 * NT)

        @block.tensor
        def _(pe):
            mm = nc.tensor.matmul

            def core_scores(T, qT_of, q_ready, q_count):
                pe.wait_ge(kblk_ready, T.count(1, 1))
                if q_ready is not None:
                    pe.wait_ge(q_ready, q_count)
                for c in range(C):
                    wait(pe, sub_done, T.count(2, c - 1))
                    for b in range(2):
                        last = mm(bank[c][64 * b:64 * b + 64, :], qT_of(c, b),
                                  kblk[:, T.two, c, b].rearrange("p h k -> p (h k)"), start=True, stop=True)
                    last.then_inc(s_made, 1)

            def core_transposes(T):
                pe.wait_ge(p_ready, T.count(1, 1))
                for half in range(2):
                    wait(pe, pT_copied, T.count(2, half - 1))
                    for j in range(4):
                        p = 4 * half + j
                        last = nc.tensor.transpose(
                            bank[2 + half][:, j * P:(j + 1) * P],
                            E[:, T.two, 2 * p:2 * p + 2].rearrange("p h k -> p (h k)"), ident)
                    last.then_inc(pT_made, 1)

            def core_heads(T, v_sem, v_count):
                pe.wait_ge(pT_copied, T.count(2, 2))
                pe.wait_ge(v_sem, v_count)
                wait(pe, o_copied, T.count(1))
                for p in range(HP):
                    c, q = p // 4, 32 * (p % 4)
                    for b in range(2):
                        last = mm(bank[4][q:q + 32, c * P + 64 * b:c * P + 64 * b + 64], vblk[:, T.two, b, p, :],
                                  PT[:, T.two, p, 64 * b:64 * b + 64], start=True, stop=True,
                                  tile_position=(0, q))
                last.then_inc(o_made, 1)

            def transpose_xn(first):
                for t in range(NT):
                    pe.wait_ge(ln_done, first + t + 1)
                    for c in range(C):
                        last = nc.tensor.transpose(bank[t][:, c * P:(c + 1) * P], xn[:, t, c * P:(c + 1) * P], ident)
                    last.then_inc(xT_made, 1)

            pe.wait_ge(ld["const"], 32)
            transpose_xn(0)
            pe.wait_ge(xT_copied, NT)
            pe.wait_ge(ld["w1"], 48)
            for m in range(C):
                for c in range(C):
                    last = mm(bank[4 + m][:, :], w1q[:, c, m * P:(m + 1) * P], xnT[:, c, :],
                              start=(c == 0), stop=(c == C - 1))
                last.then_inc(q1_made, 1)
            pe.wait_ge(q1_copied, C)
            pe.wait_ge(w1kr_ready, 1)

            def match(t):
                wait(pe, match_read, t)
                for b in range(2):
                    pe.wait_ge(ld_ctx[2 * t + b], 16)
                for half in range(M // 512):
                    for b in range(2):
                        for c in range(C):
                            last = mm(bank[6 + half][64 * b:64 * b + 64, :],
                                      q1T[:, c, t * P + 64 * b:t * P + 64 * b + 64],
                                      ctxT[:, 2 * t + b, c, half * 512:(half + 1) * 512],
                                      start=(c == 0), stop=(c == C - 1))
                last.then_inc(match_made, 1)

            def mem_transposes(t):
                pe.wait_ge(ld_mem[t], 16)
                wait(pe, k1_copied, t)
                wait(pe, v1_copied, t)
                for c in range(C):
                    last = nc.tensor.transpose(bank[5][:, c * P:(c + 1) * P], mem[:, t, c * P:(c + 1) * P], ident)
                last.then_inc(memT_made, 1)

            def kv1(t):
                pe.wait_ge(memT_copied, t + 1)
                for c in range(C):
                    mm(bank[5][:, 256:384], w1kr[:, c].rearrange("p h d -> p (h d)"),
                       memT[:, t % 2, c, :], start=(c == 0), stop=(c == C - 1))
                for b in range(2):
                    for h2 in range(2):
                        for c in range(C):
                            last = mm(bank[5][64 * h2:64 * h2 + 64, 384 + 16 * b:400 + 16 * b],
                                      memT[:, t % 2, c, 64 * b:64 * b + 64], w1kv[:, c, 16:32],
                                      start=(c == 0), stop=(c == C - 1))
                last.then_inc(kv1_made, 1)

            def scores1(t):
                core_scores(Tile(t), lambda c, b: q1T[:, c, t * P + 64 * b:t * P + 64 * b + 64], None, 0)

            def heads1(t):
                core_heads(Tile(t), v1_copied, t + 1)

            def y1(t):
                pe.wait_ge(o_copied, t + 1)
                pe.wait_ge(match_read, NT)
                for c in range(C):
                    last = mm(bank[6 + t // 2][:, D * (t % 2):D * (t % 2) + D], OT[:, t, c, :], w1c[:, c, :],
                              start=(c == 0), stop=(c == C - 1))
                last.then_inc(y_made, 1)

            match(0)
            match(1)
            mem_transposes(0)
            kv1(0)
            match(2)
            scores1(0)
            mem_transposes(1)
            kv1(1)
            match(3)
            core_transposes(Tile(0))
            scores1(1)
            mem_transposes(2)
            kv1(2)
            heads1(0)
            core_transposes(Tile(1))
            scores1(2)
            mem_transposes(3)
            kv1(3)
            heads1(1)
            y1(0)
            core_transposes(Tile(2))
            scores1(3)
            heads1(2)
            y1(1)
            core_transposes(Tile(3))
            y1(2)
            heads1(3)
            y1(3)

            transpose_xn(NT)
            pe.wait_ge(xT_copied, 2 * NT)
            outputs = [(w, h) for h in range(HP) for w in (w2q, w2k)] + [(w2v, b) for b in range(B)]
            for j, (w, k) in enumerate(outputs):
                if j == 0:
                    for name in ("w2q", "w2k", "w2v"):
                        pe.wait_ge(ld[name], 16)
                if j >= 6:
                    pe.wait_ge(p2_act if j % 2 == 0 else p2_dve, (j - 6) // 2 + 1)
                if w is w2v:
                    wide = w2v[:, :, :].rearrange("p c (h j d) -> p c h j d", h=HP, j=2)
                    for h2 in range(2):
                        for c in range(C):
                            last = mm(bank[j % 6][64 * h2:64 * h2 + 64, :], xnT[:, c, 64 * k:64 * k + 64],
                                      wide[:, c, :, h2, :], start=(c == 0), stop=(c == C - 1))
                else:
                    for c in range(C):
                        last = mm(bank[j % 6][:, :], w[:, c, k * P:(k + 1) * P], xnT[:, c, :],
                                  start=(c == 0), stop=(c == C - 1))
                last.then_inc(p2_made, 1)
            pe.wait_ge(p2_act, 12)
            pe.wait_ge(p2_dve, 12)

            def scores2(t):
                for half in range(2):
                    wait(pe, s2_masked, 2 * t + half - 1)
                    for j in range(4):
                        for b in range(2):
                            last = mm(bank[half][64 * b:64 * b + 64, j * P:(j + 1) * P],
                                      q2T[:, 4 * half + j, t * P + 64 * b:t * P + 64 * b + 64],
                                      k2blk[:, 4 * half + j, 2 * t + b].rearrange("p j k -> p (j k)"),
                                      start=True, stop=True)
                    last.then_inc(s2_made, 1)

            def transposes2(t):
                pe.wait_ge(s2_p, t + 1)
                for half in range(2):
                    wait(pe, pT2_copied, 2 * t + half - 1)
                    for j in range(4):
                        p = 4 * half + j
                        last = nc.tensor.transpose(bank[2 + half][:, j * P:(j + 1) * P],
                                                   E[:, t % 2, 2 * p:2 * p + 2].rearrange("p h k -> p (h k)"), ident)
                    last.then_inc(pT2_made, 1)

            def heads2(t, half):
                pe.wait_ge(pT2_copied, 2 * t + half + 1)
                wait(pe, o2_act, 2 * t + half)
                wait(pe, o2_dve, 2 * t + half)
                for j in range(4):
                    for b in range(2):
                        for h2 in range(2):
                            r = slice(64 * h2, 64 * h2 + 64)
                            last = mm(bank[4 + h2][r, j * P + 64 * b:j * P + 64 * b + 64],
                                      v2[r, 2 * t + b, 4 * half + j, :],
                                      PT[r, t % 2, 4 * half + j, 64 * b:64 * b + 64], start=True, stop=True,
                                      tile_position=(64 * h2, 64 * h2))
                last.then_inc(o2_made, 1)

            def y2(t):
                pe.wait_ge(o2_act, 2 * t + 2)
                pe.wait_ge(o2_dve, 2 * t + 2)
                if t == 0:
                    pe.wait_ge(ld["w2o"], 16)
                for p in range(HP):
                    last = mm(bank[6 + t // 2][:, D * (t % 2):D * (t % 2) + D], O2T[:, t % 2, p, :], w2o[:, p, :],
                              start=(p == 0), stop=(p == HP - 1))
                last.then_inc(y2_made, 1)

            scores2(0)
            scores2(1)
            transposes2(0)
            heads2(0, 0)
            heads2(0, 1)
            for t in range(1, NT):
                if t + 1 < NT:
                    scores2(t + 1)
                transposes2(t)
                y2(t - 1)
                heads2(t, 0)
                heads2(t, 1)
            y2(NT - 1)

            transpose_xn(2 * NT)
            pe.wait_ge(xT_copied, 3 * NT)
            pe.wait_ge(ld["router"], 96)
            for t in range(NT):
                for c in range(C):
                    last = mm(bank[4][:, t * P:(t + 1) * P], xnT[:, c, t * P:(t + 1) * P], rw1[:, c, :],
                              start=(c == 0), stop=(c == C - 1))
            last.then_inc(h_made, 1)

            def qk(T):
                if T.t == 0:
                    pe.wait_ge(ld_wqkv[T.weights], 16 * (T.c // 8 + 1) if T.i is None else 16 * T.i + 16 * (T.c // 8 + 1))
                wait(pe, qk_copied, T.n - CORE0)
                for j in range(2 * C):
                    w = w_of(j // C, T.weights)
                    for c in range(C):
                        last = mm(bank[5][:, j * P:(j + 1) * P], w[:, c, (j % C) * P:(j % C + 1) * P],
                                  xnT[:, c, T.t * P:(T.t + 1) * P], start=(c == 0), stop=(c == C - 1))
                last.then_inc(qk_made, 1)

            def v(T):
                wait(pe, o_copied, T.n - 1)
                wait(pe, v_copied, T.n - CORE0)
                w = w_of(2, T.weights).rearrange("p c (h j d) -> p c h j d", h=HP, j=2)
                for b in range(2):
                    for h2 in range(2):
                        for c in range(C):
                            last = mm(bank[4][64 * h2:64 * h2 + 64, b * P:(b + 1) * P],
                                      xnT[:, c, T.t * P + 64 * b:T.t * P + 64 * b + 64], w[:, c, :, h2, :],
                                      start=(c == 0), stop=(c == C - 1))
                last.then_inc(v_made, 1)

            def scores3(T):
                core_scores(T, lambda c, b: qkT[:, T.two, c, 64 * b:64 * b + 64], qk_copied, T.n - CORE0 + 1)

            def heads3(T, later_v):
                core_heads(T, v_copied, later_v)

            def y3(T):
                pe.wait_ge(o_copied, T.count(1, 1))
                if T.t == 0:
                    pe.wait_ge(ld_wo[T.weights], 16 * (T.c // 8 + 1) if T.i is None else 16 * T.i + 16 * (T.c // 8 + 1))
                for c in range(C):
                    last = mm(bank[6 + T.t // 2][:, D * (T.t % 2):D * (T.t % 2) + D], OT[:, T.t, c, :],
                              wo[:, T.weights, c, :], start=(T.i is None and T.c in (0, 2) and c == 0), stop=False,
                              skip_group_check=True)
                last.then_inc(y_made, 1)

            def step(k, i=None, bounds=(0, LAST)):
                lo, hi = bounds

                def there(s):
                    return i is not None or lo <= s < hi

                if there(k + 1):
                    qk(Tile(k + 1, i, CORE0))
                if there(k - 1):
                    v(Tile(k - 1, i, CORE0))
                if there(k - 3):
                    y3(Tile(k - 3, i, CORE0))
                if there(k):
                    scores3(Tile(k, i, CORE0))
                if there(k - 1):
                    core_transposes(Tile(k - 1, i, CORE0))
                if there(k - 2):
                    made = Tile(k, i, CORE0).n - CORE0
                    heads3(Tile(k - 2, i, CORE0), min(made, LAST) if i is None else made)

            step(-1)
            pe.wait_ge(h_ready, 1)
            for t in range(NT):
                last = nc.tensor.transpose(bank[0][:, t * P:(t + 1) * P], hid[:, t, :], ident)
            last.then_inc(hT_made, 1)
            pe.wait_ge(hT_copied, 1)
            for t in range(NT):
                last = mm(bank[1][:, NE * t:NE * t + NE], hidT[:, t * P:(t + 1) * P], rw2[:, :], start=True, stop=True)
            last.then_inc(l_made, 1)
            pe.wait_ge(gates_ready, 1)
            for t in range(NT):
                last = nc.tensor.transpose(bank[2][0:NE, t * P:(t + 1) * P], gates[:, t, :], ident)
            last.then_inc(gT_made, 1)
            pe.wait_ge(gT_copied, 1)
            for k in range(0, 6):
                step(k)
            with pe.Fori(0, 3) as i:
                for k in range(6, 14):
                    step(k, i)
            for k in range(30, LAST + 3):
                step(k)
            pe.wait_ge(ld["ob"], 16)
            for t in range(NT):
                last = mm(bank[6 + t // 2][:, D * (t % 2):D * (t % 2) + D], gatesT[:, t * P:(t + 1) * P], ob[:, :],
                          start=False, stop=True, skip_group_check=True)
            last.then_inc(y_all, 1)

        @block.scalar
        def _(act):
            def copy(dst, src):
                return nc.scalar.activation(dst, src, ACT.Copy)

            def core_exp(T):
                for c in range(2):
                    act.wait_ge(sub_done, T.count(2, c + 1))
                    part = E[:, T.two, 8 * c:8 * c + 8].rearrange("p h k -> p (h k)")
                    nc.scalar.activation(part, part, ACT.Exp).then_inc(exp_done, 1)

            def core_copy_pT(T):
                wait(act, o_made, T.count(1, -1))
                for half in range(2):
                    act.wait_ge(pT_made, T.count(2, half + 1))
                    copy(PT[:, T.two, 4 * half:4 * half + 4].rearrange("p h q -> p (h q)"),
                         bank[2 + half][:, :]).then_inc(pT_copied, 1)

            def core_copy_o(T):
                wait(act, y_made, T.count(1, -3))
                act.wait_ge(o_made, T.count(1, 1))
                copy(OT[:, T.t].rearrange("p c q -> p (c q)"), bank[4][:, 0:C * P]).then_inc(o_copied, 1)

            def copy_xT(first):
                for t in range(NT):
                    act.wait_ge(xT_made, first + t + 1)
                    copy(xnT[:, :, t * P:(t + 1) * P],
                         bank[t][:, 0:C * P].rearrange("p (c q) -> p c q", c=C)).then_inc(xT_copied, 1)

            copy_xT(0)
            for m in range(C):
                act.wait_ge(q1_made, m + 1)
                copy(q1T[:, m, :], bank[4 + m][:, :]).then_inc(q1_copied, 1)

            def copy_memT(t):
                act.wait_ge(memT_made, t + 1)
                copy(memT[:, t % 2].rearrange("p c q -> p (c q)"), bank[5][:, 0:C * P]).then_inc(memT_copied, 1)

            def copy_k1(t):
                act.wait_ge(kv1_made, t + 1)
                wait(act, kblk_ready, t - 1)
                copy(qkT[:, t % 2, C, :], bank[5][:, 256:384]).then_inc(k1_copied, 1)

            copy_memT(0)
            copy_k1(0)
            copy_memT(1)
            copy_k1(1)
            core_exp(Tile(0))
            core_copy_pT(Tile(0))
            copy_memT(2)
            copy_k1(2)
            core_exp(Tile(1))
            core_copy_o(Tile(0))
            core_copy_pT(Tile(1))
            copy_memT(3)
            copy_k1(3)
            core_exp(Tile(2))
            core_copy_o(Tile(1))
            core_copy_pT(Tile(2))
            core_exp(Tile(3))
            core_copy_o(Tile(2))
            core_copy_pT(Tile(3))
            core_copy_o(Tile(3))

            copy_xT(NT)
            for n in range(12):
                j = 2 * n
                act.wait_ge(p2_made, j + 1)
                dst = q2T[:, n, :] if n < HP else v2[:, j - 16].rearrange("p h d -> p (h d)")
                copy(dst, bank[j % 6][:, :]).then_inc(p2_act, 1)

            def exp2(t):
                for half in range(2):
                    act.wait_ge(s2_sub, 2 * t + half + 1)
                    part = E[:, t % 2, 8 * half:8 * half + 8].rearrange("p h k -> p (h k)")
                    nc.scalar.activation(part, part, ACT.Exp).then_inc(s2_exp, 1)

            def copy_pT2(t):
                wait(act, o2_made, 2 * (t - 1))
                for half in range(2):
                    act.wait_ge(pT2_made, 2 * t + half + 1)
                    copy(PT[:, t % 2, 4 * half:4 * half + 4].rearrange("p h q -> p (h q)"),
                         bank[2 + half][:, :]).then_inc(pT2_copied, 1)

            def copy_o2(t):
                wait(act, y2_made, t - 1)
                for half in range(2):
                    act.wait_ge(o2_made, 2 * t + half + 1)
                    copy(O2T[0:64, t % 2, 4 * half:4 * half + 4].rearrange("p h q -> p (h q)"),
                         bank[4][0:64, :]).then_inc(o2_act, 1)

            exp2(0)
            exp2(1)
            for t in range(NT):
                copy_pT2(t)
                copy_o2(t)
                if t + 2 < NT:
                    exp2(t + 2)

            copy_xT(2 * NT)

            def copy_qk(T):
                act.wait_ge(qk_made, T.n - CORE0 + 1)
                wait(act, s_made, T.count(2, -2))
                wait(act, kblk_ready, T.count(1, -1))
                for j in range(2 * C):
                    last = nc.scalar.activation(qkT[:, T.two, j, :], bank[5][:, j * P:(j + 1) * P], ACT.Identity,
                                                bias=wqkv[:, T.weights, 3 * C * D + j:3 * C * D + j + 1])
                last.then_inc(qk_copied, 1)

            def step(k, i=None):
                def there(s):
                    return i is not None or 0 <= s < LAST

                if there(k + 1):
                    copy_qk(Tile(k + 1, i, CORE0))
                if there(k - 1):
                    core_copy_pT(Tile(k - 1, i, CORE0))
                if there(k - 2):
                    core_copy_o(Tile(k - 2, i, CORE0))
                if there(k):
                    core_exp(Tile(k, i, CORE0))

            step(-1)
            act.wait_ge(hT_made, 1)
            nc.scalar.activation(hidT[:, :], bank[0][:, :], ACT.Relu).then_inc(hT_copied, 1)
            act.wait_ge(r_exp_in, 1)
            nc.scalar.activation(prob[:, :, :], prob[:, :, :], ACT.Exp).then_inc(r_exp, 1)
            act.wait_ge(gT_made, 1)
            copy(gatesT[:, :], bank[2][0:NE, :]).then_inc(gT_copied, 1)
            for k in range(0, 6):
                step(k)
            with act.Fori(0, 3) as i:
                for k in range(6, 14):
                    step(k, i)
            for k in range(30, LAST + 3):
                step(k)

        @block.gpsimd
        def _(pool):
            nc.gpsimd.memset(vblk[:, :, :, :, :], 0.0).then_inc(vblk_zero, 1)

            def root(group):
                ts = NORM_GROUPS[group]
                sl = slice(ts[0], ts[-1] + 1)
                pool.wait_ge(ln_mom, sum(len(g) for g in NORM_GROUPS[:group + 1]))
                nc.gpsimd.tensor_scalar(rstd[:, sl], moments[:, sl, 1], EPS, None, ALU.add).then_inc(ln_eps, 1)
                pool.wait_ge(ln_eps, group + 1)
                nc.gpsimd.tensor_tensor(rstd[:, sl], rstd[:, sl], minus_half[:, 0:len(ts)], ALU.pow)\
                  .then_inc(ln_rstd, 1)

            def scale(two, r, r_sem, r_count, done):
                pool.wait_ge(r_sem, r_count)
                nc.gpsimd.tensor_tensor(E[:, two], E[:, two], r[:, two, :].unsqueeze(2).to_broadcast([P, H, L]),
                                        ALU.mult).then_inc(done, 1)

            pool.wait_ge(ld["const"], 32)
            root(0)
            pool.wait_ge(ld["w1"], 48)
            nc.gpsimd.tensor_copy(w1kr[:, :, :, :], w1kv[:, :, 0:16].unsqueeze(2).to_broadcast([P, C, 8, 16]))\
              .then_inc(w1kr_ready, 1)
            order = [("g", 0), ("g", 1), ("g", 2), ("s", 0), ("g", 3), ("s", 1), ("s", 2), ("s", 3)]
            for what, t in order:
                if what == "g":
                    pool.wait_ge(rows_ready, t + 1)
                    pool.indirect_dma_start(
                        mem[:, t, :], None, A["ctx"],
                        bass.IndirectOffsetOnAxis(ap=rows[:, t:t + 1], axis=0)).then_inc(ld_mem[t], 16)
                else:
                    scale(t % 2, recip, recip_done, t + 1, p_ready)
            root(1)
            root(2)
            for t in range(NT):
                scale(t % 2, recip, s2_recip, t + 1, s2_p)
            root(3)
            root(4)

            def step(k, i=None):
                def there(s):
                    return i is not None or 0 <= s < LAST

                if there(k):
                    T = Tile(k, i, CORE0)
                    scale(T.two, rgate, r_ready, T.n - CORE0 + 1, p_ready)

            step(-1)
            root(5)
            for k in range(0, 6):
                step(k)
            with pool.Fori(0, 3) as i:
                for k in range(6, 14):
                    step(k, i)
            for k in range(30, LAST + 3):
                step(k)

        @block.vector
        def _(dve):
            ve = nc.vector

            def bc(ap, n):
                return ap.unsqueeze(2).to_broadcast([P, ap.shape[1], n])

            def normalise(group, ts, src, dst, done):
                before = sum(len(g) for g in NORM_GROUPS[:group])
                for j, t in enumerate(ts):
                    ve.bn_stats(stats[:, t], src(t)).then_inc(ln_stat, 1)
                for j, t in enumerate(ts):
                    dve.wait_ge(ln_stat, before + j + 1)
                    ve.bn_aggr(moments[:, t], stats[:, t]).then_inc(ln_mom, 1)
                dve.wait_ge(ln_rstd, group + 1)
                for t in ts:
                    ve.tensor_scalar(dst(t), src(t), moments[:, t, 0:1], rstd[:, t:t + 1],
                                     ALU.subtract, ALU.mult).then_inc(done, 1)

            def core_kblk(T, k_sem, k_count, shared):
                dve.wait_ge(k_sem, k_count)
                wait(dve, s_made, T.count(2, -2))
                if shared:
                    src = qkT[:, T.two, C, :].rearrange("p (b k) -> p b k", b=2).unsqueeze(1).to_broadcast([P, C, 2, L])
                else:
                    src = qkT[:, T.two, C:2 * C].rearrange("p c (b k) -> p c b k", b=2)
                for h in range(8):
                    last = ve.tensor_scalar(kblk[:, T.two, :, :, h, :], src, head_mask[:, h:h + 1], None, ALU.mult)
                last.then_inc(kblk_ready, 1)

            def core_softmax(T):
                for c in range(2):
                    dve.wait_ge(s_made, T.count(2, c + 1))
                    ve.tensor_reduce(mx[:, T.two, 8 * c:8 * c + 8], bank[c][:, :].rearrange("p (h k) -> p h k", h=8),
                                     AX.X, ALU.max).then_inc(max_done, 1)
                wait(dve, pT_made, T.count(2, -2))
                for c in range(2):
                    dve.wait_ge(max_done, T.count(2, c + 1))
                    ve.tensor_tensor(E[:, T.two, 8 * c:8 * c + 8], bank[c][:, :].rearrange("p (h k) -> p h k", h=8),
                                     bc(mx[:, T.two, 8 * c:8 * c + 8], L), ALU.subtract).then_inc(sub_done, 1)

            def core_sum(T, gated):
                wait(dve, p_ready, T.count(1, -1))
                for c in range(2):
                    dve.wait_ge(exp_done, T.count(2, c + 1))
                    ve.tensor_reduce(ssum[:, T.two, 8 * c:8 * c + 8], E[:, T.two, 8 * c:8 * c + 8], AX.X, ALU.add)\
                      .then_inc(sum_done, 1)
                dve.wait_ge(sum_done, T.count(2, 2))
                ve.reciprocal(recip[:, T.two], ssum[:, T.two]).then_inc(recip_done, 1)
                if gated:
                    dve.wait_ge(recip_done, T.count(1, 1))
                    e = T.expert
                    gate = gates[:, T.t, e:e + 1] if isinstance(e, int) else gates[:, T.t, bass.ds(e, 1)]
                    ve.tensor_scalar(rgate[:, T.two], recip[:, T.two], gate, None, ALU.mult).then_inc(r_ready, 1)

            dve.wait_ge(ld["x"], 16)
            normalise(0, NORM_GROUPS[0], lambda t: xres[:, t], lambda t: xn[:, t], ln_done)

            def search(t):
                dve.wait_ge(match_made, t + 1)
                whole = match_banks[:, :]
                ve.max(top8[:, t], whole).then_inc(match_max, 1)
                dve.wait_ge(match_max, t + 1)
                ve.max_index(top8i[:, t], top8[:, t], whole).then_inc(match_read, 1)
                dve.wait_ge(match_read, t + 1)
                ve.tensor_tensor(rows[:, t:t + 1], top8i[:, t, 0:1], row_base[:, t:t + 1], ALU.add)\
                  .then_inc(rows_ready, 1)

            def copy_v1(t):
                dve.wait_ge(k1_copied, t + 1)
                wait(dve, o_made, t - 1)
                for h2 in range(2):
                    r = slice(64 * h2, 64 * h2 + 64)
                    for b in range(2):
                        last = ve.tensor_copy(
                            vblk[r, t % 2, b, :, 16 * h2:16 * h2 + 16],
                            bank[5][r, 384 + 16 * b:400 + 16 * b].unsqueeze(1).to_broadcast([64, HP, 16]))
                last.then_inc(v1_copied, 1)

            def add_y(t, done, count):
                dve.wait_ge(done, count)
                ve.tensor_tensor(xres[:, t], bank[6 + t // 2][:, D * (t % 2):D * (t % 2) + D], xres[:, t], ALU.add)\
                  .then_inc(x_added, 1)

            dve.wait_ge(ld["const"], 32)
            dve.wait_ge(vblk_zero, 1)
            def kv(t):
                core_kblk(Tile(t), k1_copied, t + 1, True)
                copy_v1(t)

            search(0)
            search(1)
            kv(0)
            search(2)
            core_softmax(Tile(0))
            core_sum(Tile(0), False)
            kv(1)
            search(3)
            core_softmax(Tile(1))
            core_sum(Tile(1), False)
            kv(2)
            core_softmax(Tile(2))
            core_sum(Tile(2), False)
            kv(3)
            core_softmax(Tile(3))
            core_sum(Tile(3), False)
            for half in range(2):
                for t in (2 * half, 2 * half + 1):
                    add_y(t, y_made, 2 * half + 2)
                dve.wait_ge(x_added, 2 * half + 2)
                normalise(1 + half, NORM_GROUPS[1 + half], lambda t: xres[:, t], lambda t: xn[:, t], ln_done)

            for n in range(12):
                j = 2 * n + 1
                dve.wait_ge(p2_made, j + 1)
                if n < HP:
                    src = bank[j % 6][:, :].rearrange("p (b k) -> p b k", b=B)
                    for h2 in range(2):
                        last = ve.tensor_scalar(k2blk[:, n, :, h2, :], src, pair_mask[:, h2:h2 + 1], None, ALU.mult)
                else:
                    last = ve.tensor_copy(v2[:, j - 16].rearrange("p h d -> p (h d)"), bank[j % 6][:, :])
                last.then_inc(p2_dve, 1)

            def softmax2(t):
                wait(dve, pT2_made, 2 * (t - 1))
                for half in range(2):
                    hs = slice(8 * half, 8 * half + 8)
                    dve.wait_ge(s2_made, 2 * t + half + 1)
                    ve.tensor_tensor(E[:, t % 2, hs], bank[half][:, :].rearrange("p (h k) -> p h k", h=8),
                                     causal.unsqueeze(1).to_broadcast([P, 8, L]), ALU.add).then_inc(s2_masked, 1)
                for half in range(2):
                    hs = slice(8 * half, 8 * half + 8)
                    dve.wait_ge(s2_masked, 2 * t + half + 1)
                    ve.tensor_reduce(mx[:, t % 2, hs], E[:, t % 2, hs], AX.X, ALU.max).then_inc(s2_max, 1)
                for half in range(2):
                    hs = slice(8 * half, 8 * half + 8)
                    dve.wait_ge(s2_max, 2 * t + half + 1)
                    ve.tensor_tensor(E[:, t % 2, hs], E[:, t % 2, hs], bc(mx[:, t % 2, hs], L), ALU.subtract)\
                      .then_inc(s2_sub, 1)

            def sum2(t):
                wait(dve, s2_p, t - 1)
                for half in range(2):
                    hs = slice(8 * half, 8 * half + 8)
                    dve.wait_ge(s2_exp, 2 * t + half + 1)
                    ve.tensor_reduce(ssum[:, t % 2, hs], E[:, t % 2, hs], AX.X, ALU.add).then_inc(s2_sum, 1)
                dve.wait_ge(s2_sum, 2 * t + 2)
                ve.reciprocal(recip[:, t % 2], ssum[:, t % 2]).then_inc(s2_recip, 1)

            def copy_o2(t):
                wait(dve, y2_made, t - 1)
                for half in range(2):
                    dve.wait_ge(o2_made, 2 * t + half + 1)
                    ve.tensor_copy(O2T[64:128, t % 2, 4 * half:4 * half + 4].rearrange("p h q -> p (h q)"),
                                   bank[5][64:128, :]).then_inc(o2_dve, 1)

            softmax2(0)
            sum2(0)
            softmax2(1)
            sum2(1)
            for t in range(NT):
                copy_o2(t)
                if t + 2 < NT:
                    softmax2(t + 2)
                    sum2(t + 2)
            for half in range(2):
                for t in (2 * half, 2 * half + 1):
                    add_y(t, y2_made, 2 * half + 2)
                dve.wait_ge(x_added, NT + 2 * half + 2)
                normalise(3 + half, NORM_GROUPS[3 + half], lambda t: xres[:, t], lambda t: xn[:, t], ln_done)

            links = [0]

            def link(ins):
                links[0] += 1
                ins.then_inc(r_chain, 1)
                dve.wait_ge(r_chain, links[0])

            dve.wait_ge(h_made, 1)
            dve.wait_ge(ld["router"], 96)
            h_ps = bank[4][:, :].rearrange("p (t j) -> p t j", t=NT)
            link(ve.tensor_tensor(hid[:, :, :], h_ps, rb1[:, :].unsqueeze(1).to_broadcast([P, NT, P]), ALU.add))
            normalise(5, NORM_GROUPS[5], lambda t: hid[:, t], lambda t: hid[:, t], hid_normed)
            dve.wait_ge(hid_normed, NT)
            link(ve.tensor_tensor(hid[:, :, :], hid[:, :, :], lng[:, :].unsqueeze(1).to_broadcast([P, NT, P]), ALU.mult))
            ve.tensor_tensor(hid[:, :, :], hid[:, :, :], lnb[:, :].unsqueeze(1).to_broadcast([P, NT, P]), ALU.add)\
              .then_inc(h_ready, 1)
            dve.wait_ge(l_made, 1)
            l_ps = bank[1][:, 0:NT * NE].rearrange("p (t e) -> p t e", t=NT)
            link(ve.tensor_tensor(logit[:, :, :], l_ps, rb2[:, :].unsqueeze(1).to_broadcast([P, NT, NE]), ALU.add))
            link(ve.tensor_reduce(rtmp[:, 0, :], logit[:, :, :], AX.X, ALU.max))
            ve.tensor_tensor(prob[:, :, :], logit[:, :, :], bc(rtmp[:, 0, :], NE), ALU.subtract).then_inc(r_exp_in, 1)
            dve.wait_ge(r_exp, 1)
            link(ve.tensor_reduce(rtmp[:, 1, :], prob[:, :, :], AX.X, ALU.add))
            link(ve.reciprocal(rtmp[:, 2, :], rtmp[:, 1, :]))
            link(ve.tensor_tensor(prob[:, :, :], prob[:, :, :], bc(rtmp[:, 2, :], NE), ALU.mult))
            for t in range(NT):
                link(ve.max(ptop[:, t], prob[:, t]))
            for t in range(NT):
                link(ve.max_index(itop[:, t], ptop[:, t], prob[:, t]))
            link(ve.tensor_copy(itopf[:, :, :], itop[:, :, :]))
            for t in range(NT):
                for r in range(2):
                    link(ve.tensor_scalar(pick[:, r, t, :], iota, itopf[:, t, r:r + 1], ptop[:, t, r:r + 1],
                                          ALU.is_equal, ALU.mult))
            link(ve.tensor_tensor(pick[:, 0], pick[:, 0], pick[:, 1], ALU.add))
            link(ve.tensor_reduce(rtmp[:, 3, :], ptop[:, :, 0:2], AX.X, ALU.add))
            link(ve.reciprocal(rtmp[:, 1, :], rtmp[:, 3, :]))
            ve.tensor_tensor(gates[:, :, :], pick[:, 0], bc(rtmp[:, 1, :], NE), ALU.mult).then_inc(gates_ready, 1)
            dve.wait_ge(gates_ready, 1)

            def copy_v(T):
                dve.wait_ge(v_made, T.n - CORE0 + 1)
                wait(dve, o_made, T.count(1, -1))
                if T.t == 0:
                    dve.wait_ge(ld_vb[T.weights], 16 * (T.c // 8 + 1) if T.i is None else 16 * T.i + 16 * (T.c // 8 + 1))
                bias = vb[:, T.weights, :].rearrange("p (h j d) -> p h j d", h=HP, j=2)
                for h2 in range(2):
                    r = slice(64 * h2, 64 * h2 + 64)
                    last = ve.tensor_tensor(
                        vblk[r, T.two, :, :, 16 * h2:16 * h2 + 16],
                        bank[4][r, 0:2 * P].rearrange("p (b h d) -> p b h d", b=2, h=HP),
                        bias[r, :, h2, :].unsqueeze(1).to_broadcast([64, 2, HP, 16]), ALU.add)
                last.then_inc(v_copied, 1)

            def step(k, i=None):
                def there(s):
                    return i is not None or 0 <= s < LAST

                if there(k + 1):
                    T = Tile(k + 1, i, CORE0)
                    core_kblk(T, qk_copied, T.n - CORE0 + 1, False)
                if there(k - 1):
                    copy_v(Tile(k - 1, i, CORE0))
                if there(k):
                    core_softmax(Tile(k, i, CORE0))
                    core_sum(Tile(k, i, CORE0), True)

            for k in range(-1, 6):
                step(k)
            with dve.Fori(0, 3) as i:
                for k in range(6, 14):
                    step(k, i)
            for k in range(30, LAST + 3):
                step(k)
            dve.wait_ge(y_all, 1)
            for t in range(NT):
                ve.tensor_tensor(final[:, t], bank[6 + t // 2][:, D * (t % 2):D * (t % 2) + D], xres[:, t], ALU.add)\
                  .then_inc(final_ready, 1)


def kernel(**inputs):
    import numpy as np
    import concourse.bacc as bacc
    from concourse.bass_utils import run_bass_kernel_spmd

    def halves(w):
        n, k = w.shape
        return np.ascontiguousarray(w.T.reshape(k // P, P, n).transpose(1, 0, 2))

    g = {k: np.asarray(v) for k, v in inputs.items()}
    x, ctx = g["x"], g["ctx_1024"]
    b, l, d = x.shape
    m = ctx.shape[1]
    ne = g["L0_ffn_qW"].shape[0]
    a = {
        "x": np.ascontiguousarray(x.reshape(b * l, d)),
        "ctx": np.ascontiguousarray(ctx.reshape(b * m, d)),
        "ctxT": np.ascontiguousarray(ctx.transpose(0, 2, 1).reshape(b, d // P, P, m).transpose(0, 2, 1, 3)),
        "w1q": halves(g["L0_xattn_Wq"]),
        "w1kv": halves(g["L0_xattn_Wkv"]),
        "w1c": halves(g["L0_xattn_Wc"]),
        "w2q": halves(g["L0_attn_wq"]),
        "w2k": halves(g["L0_attn_wk"]),
        "w2v": halves(g["L0_attn_wv"]),
        "w2o": halves(g["L0_attn_wo"]),
        "rw1": halves(g["L0_ffn_rW1"]),
        "rw2": np.ascontiguousarray(g["L0_ffn_rW2"].T),
        "rb1": np.ascontiguousarray(g["L0_ffn_rb1"].reshape(1, -1)),
        "ln_g": np.ascontiguousarray(g["L0_ffn_ln_g"].reshape(1, -1)),
        "ln_b": np.ascontiguousarray(g["L0_ffn_ln_b"].reshape(1, -1)),
        "rb2": np.ascontiguousarray(g["L0_ffn_rb2"].reshape(1, -1)),
        "ob": np.ascontiguousarray(g["L0_ffn_ob"]),
        "vb": np.ascontiguousarray(g["L0_ffn_vb"]),
    }
    packs = []
    for e in range(ne):
        parts = [halves(g[f"L0_ffn_{n}W"][e]).reshape(P, -1) for n in "qkv"]
        parts += [g[f"L0_ffn_{n}b"][e].reshape(d // P, P).T for n in "qk"]
        packs.append(np.concatenate(parts, axis=1))
    a["w_qkv"] = np.ascontiguousarray(np.stack(packs))
    a["w_o"] = np.ascontiguousarray(np.stack([halves(g["L0_ffn_oW"][e]) for e in range(ne)]))

    row = np.arange(P)[:, None]
    const = np.concatenate([
        np.eye(P),
        0.25 * (row // 16 == np.arange(8)),
        0.125 * (row // 64 == np.arange(2)),
        np.where(np.arange(l) <= row % l, 0.0, -3e38),
        np.broadcast_to(np.arange(8), (P, 8)),
        np.full((P, 4), -0.5),
    ], axis=1).astype(np.float32)
    a["const"] = np.ascontiguousarray(const)
    a["row_base"] = np.ascontiguousarray(((2 * np.arange(4)[None, :] + row // l) * m).astype(np.uint32))

    nc = bacc.Bacc("TRN2", target_bir_lowering=False, num_devices=1)
    aps, arrays = {}, {}
    for name, v in a.items():
        arrays[f"in_{name}"] = v
        aps[name] = nc.dram_tensor(f"in_{name}", v.shape, mybir.dt.from_np(v.dtype), kind="ExternalInput").ap()
    aps["out"] = nc.dram_tensor("out_0", (b * l, d), F32, kind="ExternalOutput").ap()
    build(nc, aps)
    r = run_bass_kernel_spmd(nc, [arrays], core_ids=[0])
    return r.results[0]["out_0"].reshape(b, l, d)
```

```python
from contextlib import ExitStack

import concourse.bass as bass
from concourse import mybir

F32 = mybir.dt.float32
U32 = mybir.dt.uint32
ALU = mybir.AluOpType
ACT = mybir.ActivationFunctionType
AX = mybir.AxisListType

P = 128
EPS = 1e-5
NORM_GROUPS = [(0, 1, 2, 3), (0, 1), (2, 3), (0, 1), (0, 1), (2, 3), (2, 3)]
STAGE2_NORM, STAGE3_NORM, ROUTER_NORM = (1, 2), (3, 5), (4, 6)


class Tile:

    def __init__(self, c, i=None, first=0):
        self.c, self.i = c, i
        self.n = first + c if i is None else 8 * i + (first + c)
        self.two = c % 2
        self.t = c % 4
        self.weights = (c // 4) % 2
        self.expert = c // 4 if i is None else 2 * i + c // 4

    def count(self, per_tile, extra=0):
        return self.n * per_tile + extra


def wait(eng, sem, value):
    if isinstance(value, int) and value <= 0:
        return
    eng.wait_ge(sem, value)


def row_of(dram, e):
    return dram[e] if isinstance(e, int) else dram[bass.ds(e, 1)].squeeze(0)


WARM_UP = 4
ACT_HEADS = 3


def build(nc, A):
    x_d, out_d = A["x"], A["out"]
    NT, D, H = 4, 256, 16
    B, L, M = A["ctxT"].shape[0], 64, A["ctxT"].shape[3]
    NE = A["w_qkv"].shape[0]
    C = D // P
    HP = H // 2
    CORE0 = NT
    LAST = NT * NE

    ctx = ExitStack()
    with ctx:
        def sb(name, shape, dt=F32):
            return ctx.enter_context(nc.sbuf_tensor(name, shape, dt))

        def sem(name):
            return ctx.enter_context(nc.semaphore(name))

        pair_of_banks = [ctx.enter_context(nc.psum_tensor(f"banks{2 * i}{2 * i + 1}", [P, 1024], F32)) for i in range(4)]
        bank = [pair_of_banks[i // 2][:, 512 * (i % 2):512 * (i % 2) + 512] for i in range(8)]
        MATCH_PAIR = (3, 0, 1, 3)
        KV_BANK = (5, 4, 5, 5)
        PROJECTED = 12

        const = sb("const", [P, A["const"].shape[1]])
        ident = const[:, 0:128]
        head_mask = const[:, 128:136]
        pair_mask = const[:, 136:138]
        causal = const[:, 138:202]
        iota = const[:, 202:210]
        minus_half = const[:, 210:214]
        row_base = sb("row_base", [P, NT], U32)

        xres = sb("xres", [P, NT, D])
        xn = sb("xn", [P, NT, D])
        xnT = sb("xnT", [P, C, NT * P])
        stats = sb("stats", [P, NT, 6])
        moments = sb("moments", [P, NT, 2])
        rstd = sb("rstd", [P, NT])

        big = sb("big", [P, B * C * M])
        ctxT = big[:, :].rearrange("p (b c m) -> p b c m", b=B, c=C)
        q2T = big[:, 0:8 * 512].rearrange("p (h n) -> p h n", h=HP)
        k2blk = big[:, 4096:12288].rearrange("p (h b j k) -> p h b j k", h=HP, b=B, j=2)
        v2 = big[:, 12288:16384].rearrange("p (b h d) -> p b h d", b=B, h=HP)
        w1q = sb("w1q", [P, C, D])
        w1kv = sb("w1kv", [P, C, 32])
        w1kr = sb("w1kr", [P, C, 8, 16])
        w1c = sb("w1c", [P, C, D])
        q1T = sb("q1T", [P, C, NT * P])
        top8 = sb("top8", [P, NT, 8])
        top8i = sb("top8i", [P, NT, 8], U32)
        rows = sb("rows", [P, NT], U32)
        mem = sb("mem", [P, NT, D])
        memT = sb("memT", [P, 2, C, P])

        w2q = sb("w2q", [P, C, 1024])
        w2k = sb("w2k", [P, C, 1024])
        w2v = sb("w2v", [P, C, 1024])
        w2o = sb("w2o", [P, HP, D])
        O2T = sb("O2T", [P, 2, HP, P])

        rw1 = sb("rw1", [P, C, P])
        rw2 = sb("rw2", [P, NE])
        rb1 = sb("rb1", [P, P])
        lng = sb("lng", [P, P])
        lnb = sb("lnb", [P, P])
        rb2 = sb("rb2", [P, NE])
        hid = sb("hid", [P, NT, P])
        hidT = sb("hidT", [P, NT * P])
        logit = sb("logit", [P, NT, NE])
        prob = sb("prob", [P, NT, NE])
        rtmp = sb("rtmp", [P, 4, NT])
        ptop = sb("ptop", [P, NT, 8])
        itop = sb("itop", [P, NT, 8], U32)
        itopf = sb("itopf", [P, NT, 8])
        pick = sb("pick", [P, 2, NT, NE])
        gates = sb("gates", [P, NT, NE])
        gatesT = sb("gatesT", [NE, NT * P])
        ob = sb("ob", [NE, D])

        wqkv = sb("wqkv", [P, 2, 3 * C * D + 2 * C])
        wo = sb("wo", [P, 2, C, D])
        vb = sb("vb", [P, 2, D])

        def w_of(which, par):
            return wqkv[:, par, which * C * D:(which + 1) * C * D].rearrange("p (c n) -> p c n", c=C)

        qkT = sb("qkT", [P, 2, 2 * C, P])
        kblk = sb("kblk", [P, 2, C, 2, 8, L])
        vblk = sb("vblk", [P, 2, 2, HP, 32])
        E = sb("E", [P, 2, H, L])
        PT = sb("PT", [P, 2, HP, P])
        OT = sb("OT", [P, NT, C, P])
        mx = sb("mx", [P, 2, H])
        ssum = sb("ssum", [P, 2, H])
        recip = sb("recip", [P, 2, H])
        rgate = sb("rgate", [P, 2, H])
        final = xn

        ld = {name: sem(f"ld_{name}") for name in (
            "const", "x", "w1", "router", "w2q", "w2k", "w2v", "w2o", "ob")}
        ld_ctx = [sem(f"ld_ctx{b}") for b in range(B)]
        ld_mem = [sem(f"ld_mem{t}") for t in range(NT)]
        ld_wqkv = [sem(f"ld_wqkv{p}") for p in range(2)]
        ld_wo = [sem(f"ld_wo{p}") for p in range(2)]
        ld_vb = [sem(f"ld_vb{p}") for p in range(2)]
        stored = sem("stored")

        vblk_zero, w1kr_ready = sem("vblk_zero"), sem("w1kr_ready")
        ln_stat, ln_mom, ln_eps, ln_rstd = sem("ln_stat"), sem("ln_mom"), sem("ln_eps"), sem("ln_rstd")
        ln_done = sem("ln_done")
        xT_made, xT_copied = sem("xT_made"), sem("xT_copied")
        x_added = sem("x_added")
        q1_made, q1_copied = sem("q1_made"), sem("q1_copied")
        match_made, match_max, match_read = sem("match_made"), sem("match_max"), sem("match_read")
        rows_ready = sem("rows_ready")
        memT_made, memT_copied = sem("memT_made"), sem("memT_copied")
        kv1_made, k1_copied, v1_copied = sem("kv1_made"), sem("k1_copied"), sem("v1_copied")
        qk_made, qk_copied = sem("qk_made"), sem("qk_copied")
        kblk_dve, kblk_act = sem("kblk_dve"), sem("kblk_act")
        v_made, v_copied = sem("v_made"), sem("v_copied")
        s_made = sem("s_made")
        max_done = sem("max_done")
        sub_done = sem("sub_done")
        exp_done = sem("exp_done")
        sum_done = sem("sum_done")
        recip_done, r_ready = sem("recip_done"), sem("r_ready")
        p_ready = sem("p_ready")
        pT_made, pT_copied = sem("pT_made"), sem("pT_copied")
        o_made, o_copied = sem("o_made"), sem("o_copied")
        y_made = sem("y_made")
        p2_even, p2_odd = sem("p2_even"), sem("p2_odd")
        p2_act, p2_dve = sem("p2_act"), sem("p2_dve")
        s2_made, s2_masked, s2_max, s2_sub, s2_exp, s2_sum, s2_recip, s2_p = (
            sem(f"s2_{n}") for n in ("made", "masked", "max", "sub", "exp", "sum", "recip", "p"))
        pT2_made, pT2_copied = sem("pT2_made"), sem("pT2_copied")
        o2_made, o2_act, o2_dve = sem("o2_made"), sem("o2_act"), sem("o2_dve")
        y2_made = sem("y2_made")
        h_made, hT_made, hT_copied, l_made = sem("h_made"), sem("hT_made"), sem("hT_copied"), sem("l_made")
        r_chain, r_exp_in, r_exp = sem("r_chain"), sem("r_exp_in"), sem("r_exp")
        h_ready, hid_normed = sem("h_ready"), sem("hid_normed")
        gates_ready, gT_made, gT_copied = sem("gates_ready"), sem("gT_made"), sem("gT_copied")
        final_ready = sem("final_ready")

        def k_of(T, shared):
            if shared:
                return qkT[:, T.two, C, :].rearrange("p (b k) -> p b k", b=2).unsqueeze(1).to_broadcast([P, C, 2, L])
            return qkT[:, T.two, C:2 * C].rearrange("p c (b k) -> p c b k", b=2)

        def copied(n, source, copy, masked):
            pair, j = n // PROJECTED, n % PROJECTED
            if j >= HP:
                return copy(v2[:, 4 * pair + j - HP].rearrange("p h d -> p (h d)"), source[:, :])
            copy(q2T[:, j, D * pair:D * pair + D], source[:, 0:D])
            for h2 in range(2):
                last = masked(k2blk[:, j, 4 * pair:4 * pair + 4, h2, :], source[:, D:2 * D].rearrange("p (b k) -> p b k", b=4),
                              pair_mask[:, h2:h2 + 1])
            return last

        block = ctx.enter_context(nc.Block())

        @block.sync
        def _(sp):
            sp.dma_start(xres[:, :, :], x_d.rearrange("(t p) d -> p t d", p=P)).then_inc(ld["x"], 16)
            sp.dma_start(const[:, :], A["const"]).then_inc(ld["const"], 16)
            sp.dma_start(row_base[:, :], A["row_base"]).then_inc(ld["const"], 16)
            sp.dma_start(w1q[:, :, :], A["w1q"]).then_inc(ld["w1"], 16)
            for b in range(B):
                if b >= B - 2:
                    sp.wait_ge(ld_mem[b - (B - 2)], 16)
                sp.dma_start(ctxT[:, b], A["ctxT"][b]).then_inc(ld_ctx[b], 16)
                if b == 0:
                    sp.dma_start(w1kv[:, :, :], A["w1kv"]).then_inc(ld["w1"], 16)
                    sp.dma_start(w1c[:, :, :], A["w1c"]).then_inc(ld["w1"], 16)
            sp.wait_ge(ld_mem[NT - 1], 16)
            for name, dst in (("w2q", w2q), ("w2k", w2k), ("w2v", w2v), ("w2o", w2o)):
                sp.dma_start(dst[:, :, :], A[name]).then_inc(ld[name], 16)
            sp.dma_start(rw1[:, :, :], A["rw1"]).then_inc(ld["router"], 16)
            sp.dma_start(rw2[:, :], A["rw2"]).then_inc(ld["router"], 16)
            for dst, name in ((rb1, "rb1"), (lng, "ln_g"), (lnb, "ln_b"), (rb2, "rb2")):
                sp.dma_start(dst[:, :], A[name].partition_broadcast(P)).then_inc(ld["router"], 16)
            sp.dma_start(ob[:, :], A["ob"]).then_inc(ld["ob"], 16)

            def load_expert(e, par, before):
                wait(sp, qk_made, 4 * before)
                wait(sp, v_made, 4 * before)
                sp.dma_start(wqkv[:, par, :], row_of(A["w_qkv"], e)).then_inc(ld_wqkv[par], 16)
                wait(sp, v_copied, 4 * before)
                sp.dma_start(vb[:, par, :], row_of(A["vb"], e).unsqueeze(0).partition_broadcast(P)).then_inc(ld_vb[par], 16)
                if isinstance(before, int) and before <= 0:
                    pass
                else:
                    sp.wait_ge(y_made, 4 * before + CORE0)
                sp.dma_start(wo[:, par, :, :], row_of(A["w_o"], e)).then_inc(ld_wo[par], 16)

            load_expert(0, 0, 0)
            load_expert(1, 1, 0)
            with sp.Fori(1, NE // 2) as i:
                for par in range(2):
                    load_expert(2 * i + par, par, 2 * i + (par - 1))
            for t in range(NT):
                sp.wait_ge(final_ready, t + 1)
                sp.dma_start(out_d.rearrange("(t p) d -> t p d", p=P)[t], final[:, t, :]).then_inc(stored, 16)
            sp.wait_ge(stored, 16 * NT)

        @block.tensor
        def _(pe):
            mm = nc.tensor.matmul

            def core_scores(T, qT_of, q_ready, q_count):
                pe.wait_ge(kblk_dve, T.count(1, 1))
                pe.wait_ge(kblk_act, T.count(1, 1))
                if q_ready is not None:
                    pe.wait_ge(q_ready, q_count)
                for c in range(C):
                    wait(pe, sub_done, T.count(2, c - 1))
                    for b in range(2):
                        last = mm(bank[c][64 * b:64 * b + 64, :], qT_of(c, b),
                                  kblk[:, T.two, c, b].rearrange("p h k -> p (h k)"), start=True, stop=True)
                    last.then_inc(s_made, 1)

            def core_transposes(T):
                pe.wait_ge(p_ready, T.count(1, 1))
                for half in range(2):
                    wait(pe, pT_copied, T.count(2, half - 1))
                    for j in range(4):
                        p = 4 * half + j
                        last = nc.tensor.transpose(
                            bank[2 + half][:, j * P:(j + 1) * P],
                            E[:, T.two, 2 * p:2 * p + 2].rearrange("p h k -> p (h k)"), ident)
                    last.then_inc(pT_made, 1)

            def core_heads(T, v_sem, v_count):
                pe.wait_ge(pT_copied, T.count(2, 2))
                pe.wait_ge(v_sem, v_count)
                wait(pe, o_copied, T.count(1))
                for p in range(HP):
                    c, q = p // 4, 32 * (p % 4)
                    for b in range(2):
                        last = mm(bank[4][q:q + 32, c * P + 64 * b:c * P + 64 * b + 64], vblk[:, T.two, b, p, :],
                                  PT[:, T.two, p, 64 * b:64 * b + 64], start=True, stop=True,
                                  tile_position=(0, q))
                last.then_inc(o_made, 1)

            def transpose_xn(norm, pair, into):
                for t in (2 * pair, 2 * pair + 1):
                    pe.wait_ge(ln_done, NT * norm + t + 1)
                    for c in range(C):
                        j = C * (t % 2) + c
                        last = nc.tensor.transpose(into[:, j * P:(j + 1) * P], xn[:, t, c * P:(c + 1) * P], ident)
                last.then_inc(xT_made, 1)

            pe.wait_ge(vblk_zero, 1)
            for _ in range(WARM_UP):
                mm(bank[5][:, :], vblk[:, 0, 0].rearrange("p h d -> p (h d)")[:, 0:P],
                   vblk[:, :, :, :, :].rearrange("p t b h d -> p (t b h d)")[:, 0:512], start=True, stop=True)
            pe.wait_ge(ld["const"], 32)
            for pair in range(2):
                transpose_xn(0, pair, bank[pair])
            pe.wait_ge(xT_copied, 2)
            pe.wait_ge(ld["w1"], 48)
            for m in range(C):
                for c in range(C):
                    last = mm(bank[4 + m][:, :], w1q[:, c, m * P:(m + 1) * P], xnT[:, c, :],
                              start=(c == 0), stop=(c == C - 1))
                last.then_inc(q1_made, 1)
            pe.wait_ge(q1_copied, C)
            pe.wait_ge(w1kr_ready, 1)

            def match(t):
                if t == NT - 1:
                    pe.wait_ge(match_read, 1)
                for b in range(2):
                    pe.wait_ge(ld_ctx[2 * t + b], 16)
                for half in range(M // 512):
                    for b in range(2):
                        for c in range(C):
                            last = mm(bank[2 * MATCH_PAIR[t] + half][64 * b:64 * b + 64, :],
                                      q1T[:, c, t * P + 64 * b:t * P + 64 * b + 64],
                                      ctxT[:, 2 * t + b, c, half * 512:(half + 1) * 512],
                                      start=(c == 0), stop=(c == C - 1))
                last.then_inc(match_made, 1)

            def mem_transposes(t):
                pe.wait_ge(ld_mem[t], 16)
                if t >= 2:
                    wait(pe, k1_copied, (0, 0, 1, 3)[t])
                    wait(pe, v1_copied, (0, 0, 1, 3)[t])
                for c in range(C):
                    last = nc.tensor.transpose(bank[KV_BANK[t]][:, c * P:(c + 1) * P], mem[:, t, c * P:(c + 1) * P], ident)
                last.then_inc(memT_made, 1)

            def kv1(t):
                pe.wait_ge(memT_copied, t + 1)
                for c in range(C):
                    mm(bank[KV_BANK[t]][:, 256:384], w1kr[:, c].rearrange("p h d -> p (h d)"),
                       memT[:, t % 2, c, :], start=(c == 0), stop=(c == C - 1))
                for b in range(2):
                    for h2 in range(2):
                        for c in range(C):
                            last = mm(bank[KV_BANK[t]][64 * h2:64 * h2 + 64, 384 + 16 * b:400 + 16 * b],
                                      memT[:, t % 2, c, 64 * b:64 * b + 64], w1kv[:, c, 16:32],
                                      start=(c == 0), stop=(c == C - 1))
                last.then_inc(kv1_made, 1)

            def scores1(t):
                if t == 0:
                    pe.wait_ge(match_read, 2)
                core_scores(Tile(t), lambda c, b: q1T[:, c, t * P + 64 * b:t * P + 64 * b + 64], None, 0)

            def transposes1(t):
                if t == 0:
                    pe.wait_ge(match_read, 3)
                core_transposes(Tile(t))

            def heads1(t):
                core_heads(Tile(t), v1_copied, max(t + 1, 2))

            def y1(t):
                pe.wait_ge(o_copied, t + 1)
                pe.wait_ge(match_read, NT)
                for c in range(C):
                    last = mm(bank[6 + t // 2][:, D * (t % 2):D * (t % 2) + D], OT[:, t, c, :], w1c[:, c, :],
                              start=(c == 0), stop=(c == C - 1))
                last.then_inc(y_made, 1)

            def transpose_xn2(pair):
                if pair == 0:
                    pe.wait_ge(k1_copied, NT)
                    pe.wait_ge(v1_copied, NT)
                else:
                    pe.wait_ge(p2_act, PROJECTED // 2)
                transpose_xn(1, pair, bank[5])

            def project(n):
                pair, j = n // PROJECTED, n % PROJECTED
                if n < 2:
                    for name in ("w2q", "w2k", "w2v"):
                        pe.wait_ge(ld[name], 16)
                pe.wait_ge(xT_copied, 2 + pair + 1)
                if n % 2 == 0:
                    into, made = bank[5], p2_even
                    wait(pe, p2_act, n // 2)
                else:
                    into, made = bank[6 + pair], p2_odd
                    wait(pe, p2_dve, n // 2)
                if j < HP:
                    for i, w in enumerate((w2q, w2k)):
                        for c in range(C):
                            last = mm(into[:, D * i:D * i + D], w[:, c, j * P:(j + 1) * P],
                                      xnT[:, c, 2 * P * pair:2 * P * pair + 2 * P], start=(c == 0), stop=(c == C - 1))
                else:
                    b = 4 * pair + j - HP
                    wide = w2v[:, :, :].rearrange("p c (h j d) -> p c h j d", h=HP, j=2)
                    for h2 in range(2):
                        for c in range(C):
                            last = mm(into[64 * h2:64 * h2 + 64, :], xnT[:, c, 64 * b:64 * b + 64],
                                      wide[:, c, :, h2, :], start=(c == 0), stop=(c == C - 1))
                last.then_inc(made, 1)

            def scores2(t):
                pe.wait_ge(p2_act, PROJECTED // 2 * (t // 2 + 1))
                pe.wait_ge(p2_dve, PROJECTED // 2 * (t // 2 + 1))
                if t == 0:
                    pe.wait_ge(sub_done, 2 * NT)
                for half in range(2):
                    wait(pe, s2_masked, 2 * t + half - 1)
                    for j in range(4):
                        for b in range(2):
                            last = mm(bank[half][64 * b:64 * b + 64, j * P:(j + 1) * P],
                                      q2T[:, 4 * half + j, t * P + 64 * b:t * P + 64 * b + 64],
                                      k2blk[:, 4 * half + j, 2 * t + b].rearrange("p j k -> p (j k)"),
                                      start=True, stop=True)
                    last.then_inc(s2_made, 1)

            def transposes2(t):
                pe.wait_ge(s2_p, t + 1)
                for half in range(2):
                    wait(pe, pT2_copied, 2 * t + half - 1)
                    for j in range(4):
                        p = 4 * half + j
                        last = nc.tensor.transpose(bank[2 + half][:, j * P:(j + 1) * P],
                                                   E[:, t % 2, 2 * p:2 * p + 2].rearrange("p h k -> p (h k)"), ident)
                    last.then_inc(pT2_made, 1)

            def heads2(t, half):
                pe.wait_ge(pT2_copied, 2 * t + half + 1)
                if t + half == 0:
                    pe.wait_ge(o_copied, NT)
                wait(pe, o2_act, 2 * t + half)
                wait(pe, o2_dve, 2 * t + half)
                for j in range(4):
                    for b in range(2):
                        for h2 in range(2):
                            r = slice(64 * h2, 64 * h2 + 64)
                            last = mm(bank[4][r, j * P + 64 * b:j * P + 64 * b + 64],
                                      v2[r, 2 * t + b, 4 * half + j, :],
                                      PT[r, t % 2, 4 * half + j, 64 * b:64 * b + 64], start=True, stop=True,
                                      tile_position=(64 * h2, 64 * h2))
                last.then_inc(o2_made, 1)

            def y2(t):
                pe.wait_ge(o2_act, 2 * t + 2)
                pe.wait_ge(o2_dve, 2 * t + 2)
                if t == 0:
                    pe.wait_ge(ld["w2o"], 16)
                for p in range(HP):
                    last = mm(bank[6 + t // 2][:, D * (t % 2):D * (t % 2) + D], O2T[:, t % 2, p, :], w2o[:, p, :],
                              start=(p == 0), stop=(p == HP - 1))
                last.then_inc(y2_made, 1)

            def tile(k):
                return Tile(k, None, CORE0)

            def transpose_xn3(pair):
                transpose_xn(2, pair, bank[6 + pair])

            def router_hidden(pair):
                pe.wait_ge(xT_copied, 4 + pair + 1)
                pe.wait_ge(ld["router"], 96)
                for t in (2 * pair, 2 * pair + 1):
                    for c in range(C):
                        last = mm(bank[6 + pair][:, (t % 2) * P:(t % 2 + 1) * P], xnT[:, c, t * P:(t + 1) * P],
                                  rw1[:, c, :], start=(c == 0), stop=(c == C - 1))
                last.then_inc(h_made, 1)

            def router_transposes(pair):
                pe.wait_ge(h_ready, pair + 1)
                for t in (2 * pair, 2 * pair + 1):
                    last = nc.tensor.transpose(bank[6 + pair][:, (t % 2) * P:(t % 2 + 1) * P], hid[:, t, :], ident)
                last.then_inc(hT_made, 1)

            def router_logits(pair):
                pe.wait_ge(hT_copied, pair + 1)
                for t in (2 * pair, 2 * pair + 1):
                    last = mm(bank[6 + pair][:, D + NE * (t % 2):D + NE * (t % 2) + NE], hidT[:, t * P:(t + 1) * P],
                              rw2[:, :], start=True, stop=True)
                last.then_inc(l_made, 1)

            def gate_transposes(pair):
                pe.wait_ge(gates_ready, pair + 1)
                for t in (2 * pair, 2 * pair + 1):
                    last = nc.tensor.transpose(bank[6 + pair][0:NE, (t % 2) * P:(t % 2 + 1) * P], gates[:, t, :], ident)
                last.then_inc(gT_made, 1)

            def qk(T):
                if T.t == 0:
                    pe.wait_ge(ld_wqkv[T.weights], 16 * (T.c // 8 + 1) if T.i is None else 16 * T.i + 16 * (T.c // 8 + 1))
                if T.i is None and T.c in (0, 2):
                    pe.wait_ge(xT_copied, 4 + T.c // 2 + 1)
                wait(pe, qk_copied, T.n - CORE0)
                for j in range(2 * C):
                    w = w_of(j // C, T.weights)
                    for c in range(C):
                        last = mm(bank[5][:, j * P:(j + 1) * P], w[:, c, (j % C) * P:(j % C + 1) * P],
                                  xnT[:, c, T.t * P:(T.t + 1) * P], start=(c == 0), stop=(c == C - 1))
                last.then_inc(qk_made, 1)

            def v(T):
                wait(pe, o_copied, T.n - 1)
                wait(pe, v_copied, T.n - CORE0)
                w = w_of(2, T.weights).rearrange("p c (h j d) -> p c h j d", h=HP, j=2)
                for b in range(2):
                    for h2 in range(2):
                        for c in range(C):
                            last = mm(bank[4][64 * h2:64 * h2 + 64, b * P:(b + 1) * P],
                                      xnT[:, c, T.t * P + 64 * b:T.t * P + 64 * b + 64], w[:, c, :, h2, :],
                                      start=(c == 0), stop=(c == C - 1))
                last.then_inc(v_made, 1)

            def scores3(T):
                core_scores(T, lambda c, b: qkT[:, T.two, c, 64 * b:64 * b + 64], qk_copied, T.n - CORE0 + 1)

            def heads3(T, later_v):
                core_heads(T, v_copied, later_v)

            def y3(T):
                pe.wait_ge(o_copied, T.count(1, 1))
                if T.i is None and T.c in (0, 2):
                    pe.wait_ge(gT_copied, T.c // 2 + 1)
                if T.t == 0:
                    pe.wait_ge(ld_wo[T.weights], 16 * (T.c // 8 + 1) if T.i is None else 16 * T.i + 16 * (T.c // 8 + 1))
                for c in range(C):
                    last = mm(bank[6 + T.t // 2][:, D * (T.t % 2):D * (T.t % 2) + D], OT[:, T.t, c, :],
                              wo[:, T.weights, c, :], start=(T.i is None and T.c in (0, 2) and c == 0), stop=False,
                              skip_group_check=True)
                last.then_inc(y_made, 1)

            def step(k, i=None, bounds=(0, LAST)):
                lo, hi = bounds

                def there(s):
                    return i is not None or lo <= s < hi

                if there(k + 1):
                    qk(Tile(k + 1, i, CORE0))
                if there(k - 1):
                    v(Tile(k - 1, i, CORE0))
                if there(k - 3):
                    y3(Tile(k - 3, i, CORE0))
                if there(k):
                    scores3(Tile(k, i, CORE0))
                if there(k - 1):
                    core_transposes(Tile(k - 1, i, CORE0))
                if there(k - 2):
                    made = Tile(k, i, CORE0).n - CORE0
                    heads3(Tile(k - 2, i, CORE0), min(made, LAST) if i is None else made)

            match(0)
            match(1)
            match(2)
            mem_transposes(0)
            kv1(0)
            mem_transposes(1)
            kv1(1)
            scores1(0)
            mem_transposes(2)
            match(3)
            kv1(2)
            scores1(1)
            transposes1(0)
            scores1(2)
            heads1(0)
            transposes1(1)
            y1(0)
            heads1(1)
            mem_transposes(3)
            y1(1)
            kv1(3)
            transposes1(2)
            scores1(3)
            transpose_xn2(0)
            heads1(2)
            project(0)
            y1(2)
            project(1)
            project(2)
            project(3)
            transposes1(3)
            project(4)
            project(5)
            project(6)
            heads1(3)
            project(7)
            project(8)
            y1(3)
            project(9)
            project(10)
            project(11)
            transpose_xn2(1)
            scores2(0)
            project(12)
            project(13)
            project(14)
            scores2(1)
            project(16)
            project(15)
            project(18)
            transposes2(0)
            project(17)
            project(20)
            project(19)
            project(22)
            project(21)
            transposes2(1)
            heads2(0, 0)
            project(23)
            heads2(0, 1)
            scores2(2)
            y2(0)
            scores2(3)
            heads2(1, 0)
            heads2(1, 1)
            transposes2(2)
            y2(1)
            heads2(2, 0)
            heads2(2, 1)
            transposes2(3)
            y2(2)
            transpose_xn3(0)
            heads2(3, 0)
            router_hidden(0)
            heads2(3, 1)
            qk(tile(0))
            y2(3)
            qk(tile(1))
            scores3(tile(0))
            router_transposes(0)
            v(tile(0))
            transpose_xn3(1)
            router_logits(0)
            router_hidden(1)
            qk(tile(2))
            scores3(tile(1))
            gate_transposes(0)
            router_transposes(1)
            router_logits(1)
            core_transposes(tile(0))
            gate_transposes(1)
            for k in range(2, 6):
                step(k)
            with pe.Fori(0, 3) as i:
                for k in range(6, 14):
                    step(k, i)
            for k in range(30, LAST):
                step(k)
            pe.wait_ge(ld["ob"], 16)
            for t in range(NT):
                mm(bank[6 + t // 2][:, D * (t % 2):D * (t % 2) + D], gatesT[:, t * P:(t + 1) * P], ob[:, :],
                   start=False, stop=False, skip_group_check=True)
            for k in range(LAST, LAST + 3):
                step(k)

        @block.scalar
        def _(act):
            def copy(dst, src):
                return nc.scalar.activation(dst, src, ACT.Copy)

            def act_kblk(T, k_sem, k_count, shared):
                act.wait_ge(k_sem, k_count)
                wait(act, s_made, T.count(2, -2))
                for h in range(8 - ACT_HEADS, 8):
                    last = nc.scalar.activation(kblk[:, T.two, :, :, h, :], k_of(T, shared), ACT.Copy,
                                                scale=head_mask[:, h:h + 1])
                last.then_inc(kblk_act, 1)

            def core_exp(T):
                for c in range(2):
                    act.wait_ge(sub_done, T.count(2, c + 1))
                    part = E[:, T.two, 8 * c:8 * c + 8].rearrange("p h k -> p (h k)")
                    nc.scalar.activation(part, part, ACT.Exp).then_inc(exp_done, 1)

            def core_copy_pT(T):
                wait(act, o_made, T.count(1, -1))
                for half in range(2):
                    act.wait_ge(pT_made, T.count(2, half + 1))
                    copy(PT[:, T.two, 4 * half:4 * half + 4].rearrange("p h q -> p (h q)"),
                         bank[2 + half][:, :]).then_inc(pT_copied, 1)

            def core_copy_o(T):
                wait(act, y_made, T.count(1, -3))
                act.wait_ge(o_made, T.count(1, 1))
                copy(OT[:, T.t].rearrange("p c q -> p (c q)"), bank[4][:, 0:C * P]).then_inc(o_copied, 1)

            def copy_xT(norm, pair, source):
                act.wait_ge(xT_made, 2 * norm + pair + 1)
                copy(xnT[:, :, 2 * P * pair:2 * P * pair + 2 * P].rearrange("p c (t q) -> p c t q", t=2),
                     source[:, :].rearrange("p (t c q) -> p c t q", t=2, c=C)).then_inc(xT_copied, 1)

            for pair in range(2):
                copy_xT(0, pair, bank[pair])
            for m in range(C):
                act.wait_ge(q1_made, m + 1)
                copy(q1T[:, m, :], bank[4 + m][:, :]).then_inc(q1_copied, 1)

            def copy_memT(t):
                act.wait_ge(memT_made, t + 1)
                copy(memT[:, t % 2].rearrange("p c q -> p (c q)"), bank[KV_BANK[t]][:, 0:C * P]).then_inc(memT_copied, 1)

            def copy_k1(t):
                act.wait_ge(kv1_made, t + 1)
                wait(act, kblk_dve, t - 1)
                copy(qkT[:, t % 2, C, :], bank[KV_BANK[t]][:, 256:384]).then_inc(k1_copied, 1)

            def kblk1(t):
                act_kblk(Tile(t), k1_copied, t + 1, True)

            def copy_projected(n):
                act.wait_ge(p2_even, n // 2 + 1)
                copied(n, bank[5], copy, masked).then_inc(p2_act, 1)

            def masked(dst, src, mask):
                return nc.scalar.activation(dst, src, ACT.Copy, scale=mask)

            def exp2(t):
                for half in range(2):
                    act.wait_ge(s2_sub, 2 * t + half + 1)
                    part = E[:, t % 2, 8 * half:8 * half + 8].rearrange("p h k -> p (h k)")
                    nc.scalar.activation(part, part, ACT.Exp).then_inc(s2_exp, 1)

            def copy_pT2(t):
                wait(act, o2_made, 2 * (t - 1))
                for half in range(2):
                    act.wait_ge(pT2_made, 2 * t + half + 1)
                    copy(PT[:, t % 2, 4 * half:4 * half + 4].rearrange("p h q -> p (h q)"),
                         bank[2 + half][:, :]).then_inc(pT2_copied, 1)

            def copy_o2(t, half):
                wait(act, y2_made, t - 1)
                act.wait_ge(o2_made, 2 * t + half + 1)
                copy(O2T[0:64, t % 2, 4 * half:4 * half + 4].rearrange("p h q -> p (h q)"),
                     bank[4][0:64, :]).then_inc(o2_act, 1)

            def tile(k):
                return Tile(k, None, CORE0)

            def router_relu(pair):
                act.wait_ge(hT_made, pair + 1)
                nc.scalar.activation(hidT[:, D * pair:D * pair + D], bank[6 + pair][:, 0:D], ACT.Relu).then_inc(hT_copied, 1)

            def router_exp(pair):
                act.wait_ge(r_exp_in, pair + 1)
                part = prob[:, 2 * pair:2 * pair + 2, :]
                nc.scalar.activation(part, part, ACT.Exp).then_inc(r_exp, 1)

            def copy_gates(pair):
                act.wait_ge(gT_made, pair + 1)
                copy(gatesT[:, D * pair:D * pair + D], bank[6 + pair][0:NE, 0:D]).then_inc(gT_copied, 1)

            def copy_qk(T):
                act.wait_ge(qk_made, T.n - CORE0 + 1)
                wait(act, s_made, T.count(2, -2))
                wait(act, kblk_dve, T.count(1, -1))
                for j in range(2 * C):
                    last = nc.scalar.activation(qkT[:, T.two, j, :], bank[5][:, j * P:(j + 1) * P], ACT.Identity,
                                                bias=wqkv[:, T.weights, 3 * C * D + j:3 * C * D + j + 1])
                last.then_inc(qk_copied, 1)

            def kblk3(T):
                act_kblk(T, qk_copied, T.n - CORE0 + 1, False)

            def step(k, i=None):
                def there(s):
                    return i is not None or 0 <= s < LAST

                if there(k + 1):
                    copy_qk(Tile(k + 1, i, CORE0))
                    kblk3(Tile(k + 1, i, CORE0))
                if there(k - 1):
                    core_copy_pT(Tile(k - 1, i, CORE0))
                if there(k - 2):
                    core_copy_o(Tile(k - 2, i, CORE0))
                if there(k):
                    core_exp(Tile(k, i, CORE0))

            copy_memT(0)
            copy_k1(0)
            kblk1(0)
            copy_memT(1)
            copy_k1(1)
            kblk1(1)
            copy_memT(2)
            core_exp(Tile(0))
            copy_k1(2)
            kblk1(2)
            core_exp(Tile(1))
            core_copy_pT(Tile(0))
            core_copy_o(Tile(0))
            core_copy_pT(Tile(1))
            core_exp(Tile(2))
            core_copy_o(Tile(1))
            copy_memT(3)
            copy_k1(3)
            kblk1(3)
            core_copy_pT(Tile(2))
            copy_xT(1, 0, bank[5])
            core_copy_o(Tile(2))
            core_exp(Tile(3))
            copy_projected(0)
            copy_projected(2)
            core_copy_pT(Tile(3))
            copy_projected(4)
            copy_projected(6)
            core_copy_o(Tile(3))
            copy_projected(8)
            copy_projected(10)
            copy_xT(1, 1, bank[5])
            copy_projected(12)
            exp2(0)
            copy_projected(14)
            copy_projected(16)
            exp2(1)
            copy_projected(18)
            copy_pT2(0)
            copy_projected(20)
            copy_projected(22)
            copy_pT2(1)
            copy_o2(0, 0)
            copy_o2(0, 1)
            exp2(2)
            copy_o2(1, 0)
            copy_o2(1, 1)
            copy_pT2(2)
            exp2(3)
            copy_o2(2, 0)
            copy_o2(2, 1)
            copy_pT2(3)
            copy_xT(2, 0, bank[6 + 0])
            copy_o2(3, 0)
            copy_o2(3, 1)
            copy_qk(tile(0))
            kblk3(tile(0))
            copy_qk(tile(1))
            kblk3(tile(1))
            router_relu(0)
            copy_xT(2, 1, bank[6 + 1])
            core_exp(tile(0))
            router_exp(0)
            copy_qk(tile(2))
            kblk3(tile(2))
            copy_gates(0)
            router_relu(1)
            router_exp(1)
            core_exp(tile(1))
            core_copy_pT(tile(0))
            copy_gates(1)
            for k in range(2, 6):
                step(k)
            with act.Fori(0, 3) as i:
                for k in range(6, 14):
                    step(k, i)
            for k in range(30, LAST + 3):
                step(k)

        @block.gpsimd
        def _(pool):
            nc.gpsimd.memset(vblk[:, :, :, :, :], 0.0).then_inc(vblk_zero, 1)

            def root(group):
                ts = NORM_GROUPS[group]
                sl = slice(ts[0], ts[-1] + 1)
                pool.wait_ge(ln_mom, sum(len(g) for g in NORM_GROUPS[:group + 1]))
                nc.gpsimd.tensor_scalar(rstd[:, sl], moments[:, sl, 1], EPS, None, ALU.add).then_inc(ln_eps, 1)
                pool.wait_ge(ln_eps, group + 1)
                nc.gpsimd.tensor_tensor(rstd[:, sl], rstd[:, sl], minus_half[:, 0:len(ts)], ALU.pow)\
                  .then_inc(ln_rstd, 1)

            def scale(two, r, r_sem, r_count, done):
                pool.wait_ge(r_sem, r_count)
                nc.gpsimd.tensor_tensor(E[:, two], E[:, two], r[:, two, :].unsqueeze(2).to_broadcast([P, H, L]),
                                        ALU.mult).then_inc(done, 1)

            pool.wait_ge(ld["const"], 32)
            root(0)
            pool.wait_ge(ld["w1"], 48)
            nc.gpsimd.tensor_copy(w1kr[:, :, :, :], w1kv[:, :, 0:16].unsqueeze(2).to_broadcast([P, C, 8, 16]))\
              .then_inc(w1kr_ready, 1)
            def gather(t):
                pool.wait_ge(rows_ready, t + 1)
                pool.indirect_dma_start(
                    mem[:, t, :], None, A["ctx"],
                    bass.IndirectOffsetOnAxis(ap=rows[:, t:t + 1], axis=0)).then_inc(ld_mem[t], 16)

            for t in range(NT):
                gather(t)
            for t in range(NT - 1):
                scale(t % 2, recip, recip_done, t + 1, p_ready)
            root(STAGE2_NORM[0])
            scale((NT - 1) % 2, recip, recip_done, NT, p_ready)
            root(STAGE2_NORM[1])
            for t in range(NT):
                scale(t % 2, recip, s2_recip, t + 1, s2_p)
            for pair in range(2):
                root(STAGE3_NORM[pair])
                root(ROUTER_NORM[pair])

            def step(k, i=None):
                T = Tile(k, i, CORE0)
                scale(T.two, rgate, r_ready, T.n - CORE0 + 1, p_ready)

            for k in range(0, 6):
                step(k)
            with pool.Fori(0, 3) as i:
                for k in range(6, 14):
                    step(k, i)
            for k in range(30, LAST):
                step(k)

        @block.vector
        def _(dve):
            ve = nc.vector

            def bc(ap, n):
                return ap.unsqueeze(2).to_broadcast([P, ap.shape[1], n])

            def norm_moments(group, src):
                ts, before = NORM_GROUPS[group], sum(len(g) for g in NORM_GROUPS[:group])
                for t in ts:
                    ve.bn_stats(stats[:, t], src(t)).then_inc(ln_stat, 1)
                for j, t in enumerate(ts):
                    dve.wait_ge(ln_stat, before + j + 1)
                    ve.bn_aggr(moments[:, t], stats[:, t]).then_inc(ln_mom, 1)

            def norm_apply(group, src, dst, done):
                dve.wait_ge(ln_rstd, group + 1)
                for t in NORM_GROUPS[group]:
                    ve.tensor_scalar(dst(t), src(t), moments[:, t, 0:1], rstd[:, t:t + 1],
                                     ALU.subtract, ALU.mult).then_inc(done, 1)

            def core_kblk(T, k_sem, k_count, shared):
                dve.wait_ge(k_sem, k_count)
                wait(dve, s_made, T.count(2, -2))
                for h in range(8 - ACT_HEADS):
                    last = ve.tensor_scalar(kblk[:, T.two, :, :, h, :], k_of(T, shared), head_mask[:, h:h + 1], None,
                                            ALU.mult)
                last.then_inc(kblk_dve, 1)

            def core_softmax(T):
                for c in range(2):
                    dve.wait_ge(s_made, T.count(2, c + 1))
                    ve.tensor_reduce(mx[:, T.two, 8 * c:8 * c + 8], bank[c][:, :].rearrange("p (h k) -> p h k", h=8),
                                     AX.X, ALU.max).then_inc(max_done, 1)
                wait(dve, pT_made, T.count(2, -2))
                for c in range(2):
                    dve.wait_ge(max_done, T.count(2, c + 1))
                    ve.tensor_tensor(E[:, T.two, 8 * c:8 * c + 8], bank[c][:, :].rearrange("p (h k) -> p h k", h=8),
                                     bc(mx[:, T.two, 8 * c:8 * c + 8], L), ALU.subtract).then_inc(sub_done, 1)

            def core_sum(T, gated):
                wait(dve, p_ready, T.count(1, -1))
                for c in range(2):
                    dve.wait_ge(exp_done, T.count(2, c + 1))
                    ve.tensor_reduce(ssum[:, T.two, 8 * c:8 * c + 8], E[:, T.two, 8 * c:8 * c + 8], AX.X, ALU.add)\
                      .then_inc(sum_done, 1)
                dve.wait_ge(sum_done, T.count(2, 2))
                ve.reciprocal(recip[:, T.two], ssum[:, T.two]).then_inc(recip_done, 1)
                if gated:
                    dve.wait_ge(recip_done, T.count(1, 1))
                    e = T.expert
                    gate = gates[:, T.t, e:e + 1] if isinstance(e, int) else gates[:, T.t, bass.ds(e, 1)]
                    ve.tensor_scalar(rgate[:, T.two], recip[:, T.two], gate, None, ALU.mult).then_inc(r_ready, 1)

            dve.wait_ge(ld["x"], 16)
            norm_moments(0, lambda t: xres[:, t])
            norm_apply(0, lambda t: xres[:, t], lambda t: xn[:, t], ln_done)

            def search(t):
                dve.wait_ge(match_made, t + 1)
                whole = pair_of_banks[MATCH_PAIR[t]][:, :]
                ve.max(top8[:, t], whole).then_inc(match_max, 1)
                dve.wait_ge(match_max, t + 1)
                ve.max_index(top8i[:, t], top8[:, t], whole).then_inc(match_read, 1)
                dve.wait_ge(match_read, t + 1)
                ve.tensor_tensor(rows[:, t:t + 1], top8i[:, t, 0:1], row_base[:, t:t + 1], ALU.add)\
                  .then_inc(rows_ready, 1)

            def copy_v1(t):
                dve.wait_ge(k1_copied, t + 1)
                wait(dve, o_made, t - 1)
                for h2 in range(2):
                    r = slice(64 * h2, 64 * h2 + 64)
                    for b in range(2):
                        last = ve.tensor_copy(
                            vblk[r, t % 2, b, :, 16 * h2:16 * h2 + 16],
                            bank[KV_BANK[t]][r, 384 + 16 * b:400 + 16 * b].unsqueeze(1).to_broadcast([64, HP, 16]))
                last.then_inc(v1_copied, 1)

            def add_y(stage, pair, made):
                dve.wait_ge(made, 2 * pair + 2)
                for t in (2 * pair, 2 * pair + 1):
                    ve.tensor_tensor(xres[:, t], bank[6 + pair][:, D * (t % 2):D * (t % 2) + D], xres[:, t], ALU.add)\
                      .then_inc(x_added, 1)
                dve.wait_ge(x_added, NT * stage + 2 * pair + 2)
                norm_moments((STAGE2_NORM, STAGE3_NORM)[stage][pair], lambda t: xres[:, t])

            def norm_y(stage, pair):
                norm_apply((STAGE2_NORM, STAGE3_NORM)[stage][pair], lambda t: xres[:, t], lambda t: xn[:, t], ln_done)

            dve.wait_ge(ld["const"], 32)
            dve.wait_ge(vblk_zero, 1)
            def kblk1(t):
                core_kblk(Tile(t), k1_copied, t + 1, True)

            def copy_projected(n):
                dve.wait_ge(p2_odd, n // 2 + 1)
                copied(n, bank[6 + n // PROJECTED], ve.tensor_copy, masked).then_inc(p2_dve, 1)

            def masked(dst, src, mask):
                return ve.tensor_scalar(dst, src, mask, None, ALU.mult)

            def mask2(t):
                wait(dve, pT2_made, 2 * (t - 1))
                for half in range(2):
                    hs = slice(8 * half, 8 * half + 8)
                    dve.wait_ge(s2_made, 2 * t + half + 1)
                    ve.tensor_tensor(E[:, t % 2, hs], bank[half][:, :].rearrange("p (h k) -> p h k", h=8),
                                     causal.unsqueeze(1).to_broadcast([P, 8, L]), ALU.add).then_inc(s2_masked, 1)

            def softmax2(t):
                for half in range(2):
                    hs = slice(8 * half, 8 * half + 8)
                    dve.wait_ge(s2_masked, 2 * t + half + 1)
                    ve.tensor_reduce(mx[:, t % 2, hs], E[:, t % 2, hs], AX.X, ALU.max).then_inc(s2_max, 1)
                for half in range(2):
                    hs = slice(8 * half, 8 * half + 8)
                    dve.wait_ge(s2_max, 2 * t + half + 1)
                    ve.tensor_tensor(E[:, t % 2, hs], E[:, t % 2, hs], bc(mx[:, t % 2, hs], L), ALU.subtract)\
                      .then_inc(s2_sub, 1)

            def sum2(t):
                wait(dve, s2_p, t - 1)
                for half in range(2):
                    hs = slice(8 * half, 8 * half + 8)
                    dve.wait_ge(s2_exp, 2 * t + half + 1)
                    ve.tensor_reduce(ssum[:, t % 2, hs], E[:, t % 2, hs], AX.X, ALU.add).then_inc(s2_sum, 1)
                dve.wait_ge(s2_sum, 2 * t + 2)
                ve.reciprocal(recip[:, t % 2], ssum[:, t % 2]).then_inc(s2_recip, 1)

            def copy_o2(t, half):
                wait(dve, y2_made, t - 1)
                dve.wait_ge(o2_made, 2 * t + half + 1)
                ve.tensor_copy(O2T[64:128, t % 2, 4 * half:4 * half + 4].rearrange("p h q -> p (h q)"),
                               bank[4][64:128, :]).then_inc(o2_dve, 1)

            links = [0]

            def link(ins):
                links[0] += 1
                ins.then_inc(r_chain, 1)
                dve.wait_ge(r_chain, links[0])

            def tiles_of(pair):
                return slice(2 * pair, 2 * pair + 2)

            def router_bias(pair):
                if pair == 0:
                    dve.wait_ge(ld["router"], 96)
                dve.wait_ge(h_made, pair + 1)
                link(ve.tensor_tensor(hid[:, tiles_of(pair), :], bank[6 + pair][:, 0:D].rearrange("p (t j) -> p t j", t=2),
                                      rb1[:, :].unsqueeze(1).to_broadcast([P, 2, P]), ALU.add))
                norm_moments(ROUTER_NORM[pair], lambda t: hid[:, t])

            def router_norm(pair):
                part = hid[:, tiles_of(pair), :]
                norm_apply(ROUTER_NORM[pair], lambda t: hid[:, t], lambda t: hid[:, t], hid_normed)
                dve.wait_ge(hid_normed, 2 * pair + 2)
                link(ve.tensor_tensor(part, part, lng[:, :].unsqueeze(1).to_broadcast([P, 2, P]), ALU.mult))
                ve.tensor_tensor(part, part, lnb[:, :].unsqueeze(1).to_broadcast([P, 2, P]), ALU.add).then_inc(h_ready, 1)

            def router_max(pair):
                ts = tiles_of(pair)
                dve.wait_ge(l_made, pair + 1)
                link(ve.tensor_tensor(logit[:, ts, :], bank[6 + pair][:, D:D + 2 * NE].rearrange("p (t e) -> p t e", t=2),
                                      rb2[:, :].unsqueeze(1).to_broadcast([P, 2, NE]), ALU.add))
                link(ve.tensor_reduce(rtmp[:, 0, ts], logit[:, ts, :], AX.X, ALU.max))
                ve.tensor_tensor(prob[:, ts, :], logit[:, ts, :], bc(rtmp[:, 0, ts], NE), ALU.subtract)\
                  .then_inc(r_exp_in, 1)

            def router_gates(pair):
                ts = tiles_of(pair)
                both = (2 * pair, 2 * pair + 1)
                dve.wait_ge(r_exp, pair + 1)
                link(ve.tensor_reduce(rtmp[:, 1, ts], prob[:, ts, :], AX.X, ALU.add))
                link(ve.reciprocal(rtmp[:, 2, ts], rtmp[:, 1, ts]))
                link(ve.tensor_tensor(prob[:, ts, :], prob[:, ts, :], bc(rtmp[:, 2, ts], NE), ALU.mult))
                for t in both:
                    last = ve.max(ptop[:, t], prob[:, t])
                link(last)
                for t in both:
                    last = ve.max_index(itop[:, t], ptop[:, t], prob[:, t])
                link(last)
                link(ve.tensor_copy(itopf[:, ts, :], itop[:, ts, :]))
                for t in both:
                    for r in range(2):
                        last = ve.tensor_scalar(pick[:, r, t, :], iota, itopf[:, t, r:r + 1], ptop[:, t, r:r + 1],
                                                ALU.is_equal, ALU.mult)
                link(last)
                ve.tensor_tensor(pick[:, 0, ts], pick[:, 0, ts], pick[:, 1, ts], ALU.add)
                link(ve.tensor_reduce(rtmp[:, 3, ts], ptop[:, ts, 0:2], AX.X, ALU.add))
                link(ve.reciprocal(rtmp[:, 1, ts], rtmp[:, 3, ts]))
                ve.tensor_tensor(gates[:, ts, :], pick[:, 0, ts], bc(rtmp[:, 1, ts], NE), ALU.mult).then_inc(gates_ready, 1)
                dve.wait_ge(gates_ready, pair + 1)

            def tile(k):
                return Tile(k, None, CORE0)

            def kblk3(T):
                core_kblk(T, qk_copied, T.n - CORE0 + 1, False)

            def copy_v(T):
                dve.wait_ge(v_made, T.n - CORE0 + 1)
                wait(dve, o_made, T.count(1, -1))
                if T.t == 0:
                    dve.wait_ge(ld_vb[T.weights], 16 * (T.c // 8 + 1) if T.i is None else 16 * T.i + 16 * (T.c // 8 + 1))
                bias = vb[:, T.weights, :].rearrange("p (h j d) -> p h j d", h=HP, j=2)
                for h2 in range(2):
                    r = slice(64 * h2, 64 * h2 + 64)
                    last = ve.tensor_tensor(
                        vblk[r, T.two, :, :, 16 * h2:16 * h2 + 16],
                        bank[4][r, 0:2 * P].rearrange("p (b h d) -> p b h d", b=2, h=HP),
                        bias[r, :, h2, :].unsqueeze(1).to_broadcast([64, 2, HP, 16]), ALU.add)
                last.then_inc(v_copied, 1)

            def step(k, i=None):
                def there(s):
                    return i is not None or 0 <= s < LAST

                if there(k + 1):
                    kblk3(Tile(k + 1, i, CORE0))
                if there(k - 1):
                    copy_v(Tile(k - 1, i, CORE0))
                if there(k):
                    core_softmax(Tile(k, i, CORE0))
                    core_sum(Tile(k, i, CORE0), True)

            search(0)
            search(1)
            search(2)
            copy_v1(0)
            kblk1(0)
            copy_v1(1)
            kblk1(1)
            core_softmax(Tile(0))
            search(3)
            core_sum(Tile(0), False)
            core_softmax(Tile(1))
            kblk1(2)
            core_sum(Tile(1), False)
            core_softmax(Tile(2))
            copy_v1(2)
            core_sum(Tile(2), False)
            add_y(0, 0, y_made)
            kblk1(3)
            copy_v1(3)
            norm_y(0, 0)
            core_softmax(Tile(3))
            core_sum(Tile(3), False)
            copy_projected(1)
            copy_projected(3)
            copy_projected(5)
            copy_projected(7)
            add_y(0, 1, y_made)
            copy_projected(9)
            norm_y(0, 1)
            copy_projected(11)
            mask2(0)
            softmax2(0)
            copy_projected(13)
            sum2(0)
            mask2(1)
            softmax2(1)
            copy_projected(15)
            sum2(1)
            copy_projected(17)
            copy_projected(19)
            copy_projected(21)
            copy_o2(0, 0)
            copy_projected(23)
            copy_o2(0, 1)
            mask2(2)
            softmax2(2)
            sum2(2)
            copy_o2(1, 0)
            mask2(3)
            copy_o2(1, 1)
            softmax2(3)
            sum2(3)
            copy_o2(2, 0)
            add_y(1, 0, y2_made)
            copy_o2(2, 1)
            norm_y(1, 0)
            copy_o2(3, 0)
            router_bias(0)
            copy_o2(3, 1)
            router_norm(0)
            kblk3(tile(0))
            add_y(1, 1, y2_made)
            norm_y(1, 1)
            core_softmax(tile(0))
            router_max(0)
            kblk3(tile(1))
            router_bias(1)
            router_gates(0)
            router_norm(1)
            core_sum(tile(0), True)
            router_max(1)
            core_softmax(tile(1))
            router_gates(1)
            copy_v(tile(0))
            core_sum(tile(1), True)
            kblk3(tile(2))
            for k in range(2, 6):
                step(k)
            with dve.Fori(0, 3) as i:
                for k in range(6, 14):
                    step(k, i)
            for k in range(30, LAST + 3):
                step(k)
            for pair in range(2):
                dve.wait_ge(y_made, CORE0 + LAST - 2 + 2 * pair)
                for t in (2 * pair, 2 * pair + 1):
                    ve.tensor_tensor(final[:, t], bank[6 + pair][:, D * (t % 2):D * (t % 2) + D], xres[:, t], ALU.add)\
                      .then_inc(final_ready, 1)


def kernel(**inputs):
    import numpy as np
    import concourse.bacc as bacc
    from concourse.bass_utils import run_bass_kernel_spmd

    def halves(w):
        n, k = w.shape
        return np.ascontiguousarray(w.T.reshape(k // P, P, n).transpose(1, 0, 2))

    g = {k: np.asarray(v) for k, v in inputs.items()}
    x, ctx = g["x"], g["ctx_1024"]
    b, l, d = x.shape
    m = ctx.shape[1]
    ne = g["L0_ffn_qW"].shape[0]
    a = {
        "x": np.ascontiguousarray(x.reshape(b * l, d)),
        "ctx": np.ascontiguousarray(ctx.reshape(b * m, d)),
        "ctxT": np.ascontiguousarray(ctx.transpose(0, 2, 1).reshape(b, d // P, P, m).transpose(0, 2, 1, 3)),
        "w1q": halves(g["L0_xattn_Wq"]),
        "w1kv": halves(g["L0_xattn_Wkv"]),
        "w1c": halves(g["L0_xattn_Wc"]),
        "w2q": halves(g["L0_attn_wq"]),
        "w2k": halves(g["L0_attn_wk"]),
        "w2v": halves(g["L0_attn_wv"]),
        "w2o": halves(g["L0_attn_wo"]),
        "rw1": halves(g["L0_ffn_rW1"]),
        "rw2": np.ascontiguousarray(g["L0_ffn_rW2"].T),
        "rb1": np.ascontiguousarray(g["L0_ffn_rb1"].reshape(1, -1)),
        "ln_g": np.ascontiguousarray(g["L0_ffn_ln_g"].reshape(1, -1)),
        "ln_b": np.ascontiguousarray(g["L0_ffn_ln_b"].reshape(1, -1)),
        "rb2": np.ascontiguousarray(g["L0_ffn_rb2"].reshape(1, -1)),
        "ob": np.ascontiguousarray(g["L0_ffn_ob"]),
        "vb": np.ascontiguousarray(g["L0_ffn_vb"]),
    }
    packs = []
    for e in range(ne):
        parts = [halves(g[f"L0_ffn_{n}W"][e]).reshape(P, -1) for n in "qkv"]
        parts += [g[f"L0_ffn_{n}b"][e].reshape(d // P, P).T for n in "qk"]
        packs.append(np.concatenate(parts, axis=1))
    a["w_qkv"] = np.ascontiguousarray(np.stack(packs))
    a["w_o"] = np.ascontiguousarray(np.stack([halves(g["L0_ffn_oW"][e]) for e in range(ne)]))

    row = np.arange(P)[:, None]
    const = np.concatenate([
        np.eye(P),
        0.25 * (row // 16 == np.arange(8)),
        0.125 * (row // 64 == np.arange(2)),
        np.where(np.arange(l) <= row % l, 0.0, -3e38),
        np.broadcast_to(np.arange(8), (P, 8)),
        np.full((P, 4), -0.5),
    ], axis=1).astype(np.float32)
    a["const"] = np.ascontiguousarray(const)
    a["row_base"] = np.ascontiguousarray(((2 * np.arange(4)[None, :] + row // l) * m).astype(np.uint32))

    nc = bacc.Bacc("TRN2", target_bir_lowering=False, num_devices=1)
    aps, arrays = {}, {}
    for name, v in a.items():
        arrays[f"in_{name}"] = v
        aps[name] = nc.dram_tensor(f"in_{name}", v.shape, mybir.dt.from_np(v.dtype), kind="ExternalInput").ap()
    aps["out"] = nc.dram_tensor("out_0", (b * l, d), F32, kind="ExternalOutput").ap()
    build(nc, aps)
    r = run_bass_kernel_spmd(nc, [arrays], core_ids=[0])
    return r.results[0]["out_0"].reshape(b, l, d)
```

```python
from contextlib import ExitStack

import concourse.bass as bass
from concourse import mybir

F32 = mybir.dt.float32
F32R = mybir.dt.float32r
U32 = mybir.dt.uint32
ALU = mybir.AluOpType
ACT = mybir.ActivationFunctionType
AX = mybir.AxisListType

P = 128
EPS = 1e-5
NORM_GROUPS = [(0, 1), (2, 3), (0, 1), (2, 3), (0, 1), (0, 1), (2, 3), (2, 3)]
STAGE_NORM = ((0, 1), (2, 3), (4, 6))
ROUTER_NORM = (5, 7)


class Tile:

    def __init__(self, c, i=None, first=0):
        self.c, self.i = c, i
        self.n = first + c if i is None else 8 * i + (first + c)
        self.two = c % 2
        self.pair = (c // 2) % 2
        self.t = c % 4
        self.weights = (c // 4) % 2
        self.expert = c // 4 if i is None else 2 * i + c // 4

    def count(self, per_tile, extra=0):
        return self.n * per_tile + extra

    def loads(self):
        return 16 * (self.c // 8 + 1) if self.i is None else 16 * self.i + 16 * (self.c // 8 + 1)

    def of_expert(self, extra):
        return 3 * (self.c // 4) + extra if self.i is None else 6 * self.i + (3 * (self.c // 4) + extra)


def wait(eng, sem, value):
    if isinstance(value, int) and value <= 0:
        return
    eng.wait_ge(sem, value)


def row_of(dram, e):
    return dram[e] if isinstance(e, int) else dram[bass.ds(e, 1)].squeeze(0)


WARM_UP = 3
ACT_HEADS = 3


def build(nc, A):
    x_d, out_d = A["x"], A["out"]
    NT, D, H = 4, 256, 16
    B, L, M = A["ctxT"].shape[0], 64, A["ctxT"].shape[3]
    NE = A["w_qk"].shape[0]
    C = D // P
    HP = H // 2
    CORE0 = NT
    LAST = NT * NE
    LOOPS = 2

    ctx = ExitStack()
    with ctx:
        def sb(name, shape, dt=F32):
            return ctx.enter_context(nc.sbuf_tensor(name, shape, dt))

        def sem(name):
            return ctx.enter_context(nc.semaphore(name))

        pair_of_banks = [ctx.enter_context(nc.psum_tensor(f"banks{2 * i}{2 * i + 1}", [P, 1024], F32)) for i in range(4)]
        bank = [pair_of_banks[i // 2][:, 512 * (i % 2):512 * (i % 2) + 512] for i in range(8)]
        MATCH_PAIR = (3, 0, 1, 3)
        KV_BANK = (5, 4, 5, 5)
        PROJECTED = 12

        const = sb("const", [P, A["const"].shape[1]])
        ident = const[:, 0:128]
        head_mask = const[:, 128:136]
        pair_mask = const[:, 136:138]
        causal = const[:, 138:202]
        iota = const[:, 202:210]
        minus_half = const[:, 210:214]
        row_base = sb("row_base", [P, NT], U32)

        xres = sb("xres", [P, NT, D])
        xn = sb("xn", [P, NT, D])
        xnT = sb("xnT", [P, C, NT * P])
        stats = sb("stats", [P, NT, 6])
        moments = sb("moments", [P, NT, 2])
        rstd = sb("rstd", [P, NT])

        w1q = sb("w1q", [P, C, D])
        w1kv = sb("w1kv", [P, C, 32])
        w1kr = sb("w1kr", [P, C, 8, 16])
        w1c = sb("w1c", [P, C, D])
        q1T = sb("q1T", [P, C, NT * P])
        top8 = sb("top8", [P, NT, 8])
        top8i = sb("top8i", [P, NT, 8], U32)
        rows = sb("rows", [P, NT], U32)
        mem = sb("mem", [P, NT, D])
        asked = sb("asked", [P, NT])
        memT = sb("memT", [P, 2, C, P])

        w2o = sb("w2o", [P, HP, D])
        O2T = sb("O2T", [P, 2, HP, P])

        rw1 = sb("rw1", [P, C, P])
        rw2 = sb("rw2", [P, NE])
        rb1 = sb("rb1", [P, P])
        lng = sb("lng", [P, P])
        lnb = sb("lnb", [P, P])
        rb2 = sb("rb2", [P, NE])
        hid = sb("hid", [P, NT, P])
        hidT = sb("hidT", [P, NT * P])
        logit = sb("logit", [P, NT, NE])
        prob = sb("prob", [P, NT, NE])
        rtmp = sb("rtmp", [P, 4, NT])
        ptop = sb("ptop", [P, NT, 8])
        itop = sb("itop", [P, NT, 8], U32)
        itopf = sb("itopf", [P, NT, 8])
        pick = sb("pick", [P, 2, NT, NE])
        gates = sb("gates", [P, NT, NE])
        gatesT = sb("gatesT", [NE, NT * P])
        ob = sb("ob", [NE, D])

        wqk = sb("wqk", [P, 2, 2 * C * D + 2 * C])
        wv = sb("wv", [P, 2, C, D])
        wo = sb("wo", [P, 2, C, D])
        vb = sb("vb", [P, 2, D])

        def w_of(which, par):
            if which == 2:
                return wo[:, par]
            return wqk[:, par, which * C * D:(which + 1) * C * D].rearrange("p (c n) -> p c n", c=C)

        k1T = sb("k1T", [P, 2, P])
        qT = q1T[:, :, :].rearrange("p a (c n) -> p a c n", c=C)
        kT = mem[:, :, :].rearrange("p (a c) n -> p a c n", a=2)
        kblk = sb("kblk", [P, 2, C, 2, 8, L])
        vblk = sb("vblk", [P, 2, 2, HP, 32])
        E = sb("E", [P, 2, H, L])
        PT = sb("PT", [P, 2, HP, P])
        OT = sb("OT", [P, NT, C, P])
        mx = sb("mx", [P, 2, H])
        ssum = sb("ssum", [P, 2, H])
        recip = sb("recip", [P, 2, H])
        rgate = sb("rgate", [P, 2, H])
        final = xn

        w2q = sb("w2q", [P, C, 1024])
        w2k = sb("w2k", [P, C, 1024])
        w2v = sb("w2v", [P, C, 1024])

        with ExitStack() as stages_1_2:
            big = stages_1_2.enter_context(nc.sbuf_tensor("big", [P, B * C * M], F32))
        ctxT = big[:, :].rearrange("p (b c m) -> p b c m", b=B, c=C)
        q2T = big[:, 0:8 * 512].rearrange("p (h n) -> p h n", h=HP)
        k2blk = big[:, 4096:12288].rearrange("p (h b j k) -> p h b j k", h=HP, b=B, j=2)
        v2 = big[:, 12288:16384].rearrange("p (b h d) -> p b h d", b=B, h=HP)
        w_hi = sb("w_hi", [P, 3, 2, C, D], F32R)
        w_lo = sb("w_lo", [P, 3, 2, C, D], F32R)
        x_hi = sb("x_hi", [P, C, NT * P], F32R)
        x_lo = sb("x_lo", [P, C, NT * P], F32R)
        O_hi = sb("O_hi", [P, NT, C, P], F32R)
        O_lo = sb("O_lo", [P, NT, C, P], F32R)

        ld = {name: sem(f"ld_{name}") for name in (
            "const", "row_base", "w1q", "w1kv", "w1c", "router", "w2q", "w2k", "w2v", "w2o", "ob")}
        ld_x = [sem(f"ld_x{pair}") for pair in range(2)]
        ld_ctx = [sem(f"ld_ctx{b}") for b in range(B)]
        ld_mem = [sem(f"ld_mem{t}") for t in range(NT)]
        ld_wqk = [sem(f"ld_wqk{p}") for p in range(2)]
        ld_wv = [sem(f"ld_wv{p}") for p in range(2)]
        ld_wo = [sem(f"ld_wo{p}") for p in range(2)]
        ld_vb = [sem(f"ld_vb{p}") for p in range(2)]
        stored = sem("stored")

        vblk_zero, w1kr_ready = sem("vblk_zero"), sem("w1kr_ready")
        ln_stat, ln_mom, ln_eps, ln_rstd = sem("ln_stat"), sem("ln_mom"), sem("ln_eps"), sem("ln_rstd")
        ln_done = sem("ln_done")
        xT_made, xT_copied = sem("xT_made"), sem("xT_copied")
        x_added = sem("x_added")
        q1_made, q1_copied = sem("q1_made"), sem("q1_copied")
        match_made, match_max, match_read = sem("match_made"), sem("match_max"), sem("match_read")
        rows_ready = sem("rows_ready")
        rows_asked = sem("rows_asked")
        memT_made, memT_copied = sem("memT_made"), sem("memT_copied")
        kv1_made, k1_copied, v1_copied = sem("kv1_made"), sem("k1_copied"), sem("v1_copied")
        x_hi_made, x_lo_made = sem("x_hi_made"), sem("x_lo_made")
        w_hi_made, w_lo_made = sem("w_hi_made"), sem("w_lo_made")
        o_lo_made = sem("o_lo_made")
        qk_made, qk_copied = sem("qk_made"), sem("qk_copied")
        kblk_dve, kblk_act = sem("kblk_dve"), sem("kblk_act")
        v_made, v_copied = sem("v_made"), sem("v_copied")
        s_made = sem("s_made")
        max_done = sem("max_done")
        sub_done = sem("sub_done")
        exp_done = sem("exp_done")
        sum_done = sem("sum_done")
        recip_done, r_ready = sem("recip_done"), sem("r_ready")
        p_ready = sem("p_ready")
        pT_made, pT_copied = sem("pT_made"), sem("pT_copied")
        o_made, o_copied = sem("o_made"), sem("o_copied")
        y_made = sem("y_made")
        p2_even, p2_odd = sem("p2_even"), sem("p2_odd")
        p2_act, p2_dve = sem("p2_act"), sem("p2_dve")
        s2_made, s2_masked, s2_max, s2_sub, s2_exp, s2_sum, s2_recip, s2_p = (
            sem(f"s2_{n}") for n in ("made", "masked", "max", "sub", "exp", "sum", "recip", "p"))
        pT2_made, pT2_copied = sem("pT2_made"), sem("pT2_copied")
        o2_made, o2_act, o2_dve = sem("o2_made"), sem("o2_act"), sem("o2_dve")
        y2_made = sem("y2_made")
        h_made, hT_made, hT_copied, l_made = sem("h_made"), sem("hT_made"), sem("hT_copied"), sem("l_made")
        r_chain, r_exp_in, r_exp = sem("r_chain"), sem("r_exp_in"), sem("r_exp")
        h_ready, hid_normed = sem("h_ready"), sem("hid_normed")
        gates_ready, gT_made, gT_copied = sem("gates_ready"), sem("gT_made"), sem("gT_copied")
        final_ready = sem("final_ready")

        def k_of(T, shared):
            if shared:
                return k1T[:, T.two, :].rearrange("p (b k) -> p b k", b=2).unsqueeze(1).to_broadcast([P, C, 2, L])
            own = slice(P * T.two, P * T.two + P)
            return kT[:, T.pair, :, own].rearrange("p c (b k) -> p c b k", b=2)

        def copied(n, source, copy, masked):
            pair, j = n // PROJECTED, n % PROJECTED
            if j >= HP:
                return copy(v2[:, 4 * pair + j - HP].rearrange("p h d -> p (h d)"), source[:, :])
            copy(q2T[:, j, D * pair:D * pair + D], source[:, 0:D])
            for h2 in range(2):
                last = masked(k2blk[:, j, 4 * pair:4 * pair + 4, h2, :], source[:, D:2 * D].rearrange("p (b k) -> p b k", b=4),
                              pair_mask[:, h2:h2 + 1])
            return last

        block = ctx.enter_context(nc.Block())

        @block.sync
        def _(sp):
            def load_x(pair):
                ts = slice(2 * pair, 2 * pair + 2)
                sp.dma_start(xres[:, ts, :], x_d.rearrange("(t p) d -> p t d", p=P)[:, ts, :]).then_inc(ld_x[pair], 16)

            load_x(0)
            sp.dma_start(const[:, :], A["const"]).then_inc(ld["const"], 16)
            load_x(1)
            sp.dma_start(w1q[:, :, :], A["w1q"]).then_inc(ld["w1q"], 16)
            for b in range(B):
                if b == 5:
                    sp.wait_ge(rows_asked, 1)
                if b == 7:
                    sp.wait_ge(rows_asked, 2)
                sp.dma_start(ctxT[:, b], A["ctxT"][b]).then_inc(ld_ctx[b], 16)
                if b == 0:
                    sp.dma_start(row_base[:, :], A["row_base"]).then_inc(ld["row_base"], 16)
                    sp.dma_start(w1kv[:, :, :], A["w1kv"]).then_inc(ld["w1kv"], 16)
            sp.dma_start(w1c[:, :, :], A["w1c"]).then_inc(ld["w1c"], 16)
            sp.wait_ge(ld_mem[NT - 1], 16)
            for name, dst in (("w2q", w2q), ("w2k", w2k), ("w2v", w2v), ("w2o", w2o)):
                sp.dma_start(dst[:, :, :], A[name]).then_inc(ld[name], 16)
            sp.dma_start(rw1[:, :, :], A["rw1"]).then_inc(ld["router"], 16)
            sp.dma_start(rw2[:, :], A["rw2"]).then_inc(ld["router"], 16)
            for dst, name in ((rb1, "rb1"), (lng, "ln_g"), (lnb, "ln_b"), (rb2, "rb2")):
                sp.dma_start(dst[:, :], A[name].partition_broadcast(P)).then_inc(ld["router"], 16)
            sp.dma_start(ob[:, :], A["ob"]).then_inc(ld["ob"], 16)

            def load_expert(e, par, before):
                wait(sp, qk_copied, 4 * before)
                sp.dma_start(wqk[:, par, :], row_of(A["w_qk"], e)).then_inc(ld_wqk[par], 16)
                wait(sp, v_made, 4 * before)
                sp.dma_start(wv[:, par, :, :], row_of(A["w_v"], e)).then_inc(ld_wv[par], 16)
                wait(sp, v_copied, 4 * before)
                sp.dma_start(vb[:, par, :], row_of(A["vb"], e).unsqueeze(0).partition_broadcast(P)).then_inc(ld_vb[par], 16)
                sp.dma_start(wo[:, par, :, :], row_of(A["w_o"], e)).then_inc(ld_wo[par], 16)

            load_expert(0, 0, 0)
            load_expert(1, 1, 0)
            with sp.Fori(1, NE // 2) as i:
                for par in range(2):
                    load_expert(2 * i + par, par, 2 * i + (par - 1))
            for t in range(NT):
                sp.wait_ge(final_ready, t + 1)
                sp.dma_start(out_d.rearrange("(t p) d -> t p d", p=P)[t], final[:, t, :]).then_inc(stored, 16)
            sp.wait_ge(stored, 16 * NT)

        @block.tensor
        def _(pe):
            mm = nc.tensor.matmul

            def core_scores(T, qT_of, q_ready, q_count):
                pe.wait_ge(kblk_dve, T.count(1, 1))
                pe.wait_ge(kblk_act, T.count(1, 1))
                if q_ready is not None:
                    pe.wait_ge(q_ready, q_count)
                for c in range(C):
                    wait(pe, sub_done, T.count(2, c - 1))
                    for b in range(2):
                        last = mm(bank[c][64 * b:64 * b + 64, :], qT_of(c, b),
                                  kblk[:, T.two, c, b].rearrange("p h k -> p (h k)"), start=True, stop=True)
                    last.then_inc(s_made, 1)

            def core_transposes(T):
                pe.wait_ge(p_ready, T.count(1, 1))
                for half in range(2):
                    wait(pe, pT_copied, T.count(2, half - 1))
                    for j in range(4):
                        p = 4 * half + j
                        last = nc.tensor.transpose(
                            bank[2 + half][:, j * P:(j + 1) * P],
                            E[:, T.two, 2 * p:2 * p + 2].rearrange("p h k -> p (h k)"), ident)
                    last.then_inc(pT_made, 1)

            def core_heads(T, v_sem, v_count):
                pe.wait_ge(pT_copied, T.count(2, 2))
                pe.wait_ge(v_sem, v_count)
                wait(pe, o_copied, T.count(1))
                for p in range(HP):
                    c, q = p // 4, 32 * (p % 4)
                    for b in range(2):
                        last = mm(bank[4][q:q + 32, c * P + 64 * b:c * P + 64 * b + 64], vblk[:, T.two, b, p, :],
                                  PT[:, T.two, p, 64 * b:64 * b + 64], start=True, stop=True,
                                  tile_position=(0, q))
                last.then_inc(o_made, 1)

            def transpose_xn(norm, pair, into):
                for t in (2 * pair, 2 * pair + 1):
                    pe.wait_ge(ln_done, NT * norm + t + 1)
                    for c in range(C):
                        j = C * (t % 2) + c
                        last = nc.tensor.transpose(into[:, j * P:(j + 1) * P], xn[:, t, c * P:(c + 1) * P], ident)
                last.then_inc(xT_made, 1)

            def keep_warm(n, into, left, right):
                for _ in range(n):
                    mm(into[:, :], left, right, start=True, stop=True)

            pe.wait_ge(vblk_zero, 1)
            zeros = vblk[:, :, :, :, :].rearrange("p t b h d -> p (t b h d)")
            keep_warm(WARM_UP, bank[2], zeros[:, 0:P], zeros[:, 0:512])
            some = w1q[:, :, :].rearrange("p c n -> p (c n)")
            pe.wait_ge(ld["const"], 16)

            def transpose_xn1(pair):
                transpose_xn(0, pair, bank[pair])

            def project1(pair):
                pe.wait_ge(xT_copied, pair + 1)
                pe.wait_ge(ld["w1q"], 16)
                for m in range(C):
                    for c in range(C):
                        last = mm(bank[4 + pair][:, m * D:(m + 1) * D], w1q[:, c, m * P:(m + 1) * P],
                                  xnT[:, c, D * pair:D * pair + D], start=(c == 0), stop=(c == C - 1))
                last.then_inc(q1_made, 1)

            def match(t):
                if t == NT - 1:
                    pe.wait_ge(match_read, 1)
                pe.wait_ge(q1_copied, t // 2 + 1)
                for b in range(2):
                    pe.wait_ge(ld_ctx[2 * t + b], 16)
                for half in range(M // 512):
                    for b in range(2):
                        for c in range(C):
                            last = mm(bank[2 * MATCH_PAIR[t] + half][64 * b:64 * b + 64, :],
                                      q1T[:, c, t * P + 64 * b:t * P + 64 * b + 64],
                                      ctxT[:, 2 * t + b, c, half * 512:(half + 1) * 512],
                                      start=(c == 0), stop=(c == C - 1))
                last.then_inc(match_made, 1)

            def mem_transposes(t):
                pe.wait_ge(ld_mem[t], 16)
                if t < 2:
                    pe.wait_ge(q1_copied, 2)
                else:
                    wait(pe, k1_copied, (0, 0, 1, 3)[t])
                    wait(pe, v1_copied, (0, 0, 1, 3)[t])
                for c in range(C):
                    last = nc.tensor.transpose(bank[KV_BANK[t]][:, c * P:(c + 1) * P], mem[:, t, c * P:(c + 1) * P], ident)
                last.then_inc(memT_made, 1)

            def kv1(t):
                if t == 0:
                    pe.wait_ge(w1kr_ready, 1)
                    pe.wait_ge(ld["w1kv"], 16)
                pe.wait_ge(memT_copied, t + 1)
                for c in range(C):
                    mm(bank[KV_BANK[t]][:, 256:384], w1kr[:, c].rearrange("p h d -> p (h d)"),
                       memT[:, t % 2, c, :], start=(c == 0), stop=(c == C - 1))
                for b in range(2):
                    for h2 in range(2):
                        for c in range(C):
                            last = mm(bank[KV_BANK[t]][64 * h2:64 * h2 + 64, 384 + 16 * b:400 + 16 * b],
                                      memT[:, t % 2, c, 64 * b:64 * b + 64], w1kv[:, c, 16:32],
                                      start=(c == 0), stop=(c == C - 1))
                last.then_inc(kv1_made, 1)

            def scores1(t):
                if t == 0:
                    pe.wait_ge(match_read, 2)
                core_scores(Tile(t), lambda c, b: q1T[:, c, t * P + 64 * b:t * P + 64 * b + 64], None, 0)

            def transposes1(t):
                if t == 0:
                    pe.wait_ge(match_read, 3)
                core_transposes(Tile(t))

            def heads1(t):
                core_heads(Tile(t), v1_copied, max(t + 1, 2))

            def y1(t):
                if t == 0:
                    pe.wait_ge(ld["w1c"], 16)
                pe.wait_ge(o_copied, t + 1)
                pe.wait_ge(match_read, NT)
                for c in range(C):
                    last = mm(bank[6 + t // 2][:, D * (t % 2):D * (t % 2) + D], OT[:, t, c, :], w1c[:, c, :],
                              start=(c == 0), stop=(c == C - 1))
                last.then_inc(y_made, 1)

            def transpose_xn2(pair):
                if pair == 0:
                    pe.wait_ge(k1_copied, NT)
                    pe.wait_ge(v1_copied, NT)
                else:
                    pe.wait_ge(p2_act, PROJECTED // 2)
                transpose_xn(1, pair, bank[5])

            def project(n):
                pair, j = n // PROJECTED, n % PROJECTED
                if n < 2:
                    for name in ("w2q", "w2k", "w2v"):
                        pe.wait_ge(ld[name], 16)
                pe.wait_ge(xT_copied, 2 + pair + 1)
                if n % 2 == 0:
                    into, made = bank[5], p2_even
                    wait(pe, p2_act, n // 2)
                else:
                    into, made = bank[6 + pair], p2_odd
                    wait(pe, p2_dve, n // 2)
                if j < HP:
                    for i, w in enumerate((w2q, w2k)):
                        for c in range(C):
                            last = mm(into[:, D * i:D * i + D], w[:, c, j * P:(j + 1) * P],
                                      xnT[:, c, 2 * P * pair:2 * P * pair + 2 * P], start=(c == 0), stop=(c == C - 1))
                else:
                    b = 4 * pair + j - HP
                    wide = w2v[:, :, :].rearrange("p c (h j d) -> p c h j d", h=HP, j=2)
                    for h2 in range(2):
                        for c in range(C):
                            last = mm(into[64 * h2:64 * h2 + 64, :], xnT[:, c, 64 * b:64 * b + 64],
                                      wide[:, c, :, h2, :], start=(c == 0), stop=(c == C - 1))
                last.then_inc(made, 1)

            def scores2(t):
                pe.wait_ge(p2_act, PROJECTED // 2 * (t // 2 + 1))
                pe.wait_ge(p2_dve, PROJECTED // 2 * (t // 2 + 1))
                if t == 0:
                    pe.wait_ge(sub_done, 2 * NT)
                for half in range(2):
                    wait(pe, s2_masked, 2 * t + half - 1)
                    for j in range(4):
                        for b in range(2):
                            last = mm(bank[half][64 * b:64 * b + 64, j * P:(j + 1) * P],
                                      q2T[:, 4 * half + j, t * P + 64 * b:t * P + 64 * b + 64],
                                      k2blk[:, 4 * half + j, 2 * t + b].rearrange("p j k -> p (j k)"),
                                      start=True, stop=True)
                    last.then_inc(s2_made, 1)

            def transposes2(t):
                pe.wait_ge(s2_p, t + 1)
                for half in range(2):
                    wait(pe, pT2_copied, 2 * t + half - 1)
                    for j in range(4):
                        p = 4 * half + j
                        last = nc.tensor.transpose(bank[2 + half][:, j * P:(j + 1) * P],
                                                   E[:, t % 2, 2 * p:2 * p + 2].rearrange("p h k -> p (h k)"), ident)
                    last.then_inc(pT2_made, 1)

            def heads2(t, half):
                pe.wait_ge(pT2_copied, 2 * t + half + 1)
                if t + half == 0:
                    pe.wait_ge(o_copied, NT)
                wait(pe, o2_act, 2 * t + half)
                wait(pe, o2_dve, 2 * t + half)
                for j in range(4):
                    for b in range(2):
                        for h2 in range(2):
                            r = slice(64 * h2, 64 * h2 + 64)
                            last = mm(bank[4][r, j * P + 64 * b:j * P + 64 * b + 64],
                                      v2[r, 2 * t + b, 4 * half + j, :],
                                      PT[r, t % 2, 4 * half + j, 64 * b:64 * b + 64], start=True, stop=True,
                                      tile_position=(64 * h2, 64 * h2))
                last.then_inc(o2_made, 1)

            def y2(t):
                pe.wait_ge(o2_act, 2 * t + 2)
                pe.wait_ge(o2_dve, 2 * t + 2)
                if t == 0:
                    pe.wait_ge(ld["w2o"], 16)
                for p in range(HP):
                    last = mm(bank[6 + t // 2][:, D * (t % 2):D * (t % 2) + D], O2T[:, t % 2, p, :], w2o[:, p, :],
                              start=(p == 0), stop=(p == HP - 1))
                last.then_inc(y2_made, 1)

            def tile(k):
                return Tile(k, None, CORE0)

            def transpose_xn3(pair):
                transpose_xn(2, pair, bank[6 + pair])

            def router_hidden(pair):
                pe.wait_ge(x_hi_made, pair + 1)
                pe.wait_ge(ld["router"], 96)
                for t in (2 * pair, 2 * pair + 1):
                    for c in range(C):
                        last = mm(bank[6 + pair][:, (t % 2) * P:(t % 2 + 1) * P], xnT[:, c, t * P:(t + 1) * P],
                                  rw1[:, c, :], start=(c == 0), stop=(c == C - 1))
                last.then_inc(h_made, 1)

            def router_transposes(pair):
                pe.wait_ge(h_ready, pair + 1)
                for t in (2 * pair, 2 * pair + 1):
                    last = nc.tensor.transpose(bank[6 + pair][:, (t % 2) * P:(t % 2 + 1) * P], hid[:, t, :], ident)
                last.then_inc(hT_made, 1)

            def router_logits(pair):
                pe.wait_ge(hT_copied, pair + 1)
                for t in (2 * pair, 2 * pair + 1):
                    last = mm(bank[6 + pair][:, D + NE * (t % 2):D + NE * (t % 2) + NE], hidT[:, t * P:(t + 1) * P],
                              rw2[:, :], start=True, stop=True)
                last.then_inc(l_made, 1)

            def gate_transposes(pair):
                pe.wait_ge(gates_ready, pair + 1)
                for t in (2 * pair, 2 * pair + 1):
                    last = nc.tensor.transpose(bank[6 + pair][0:NE, (t % 2) * P:(t % 2 + 1) * P], gates[:, t, :], ident)
                last.then_inc(gT_made, 1)

            def qk(T):
                which = T.c % 2
                if T.t < 2:
                    pe.wait_ge(w_lo_made, T.of_expert(which + 1))
                if T.i is None and T.c in (0, 2):
                    pe.wait_ge(x_lo_made, T.c // 2 + 1)
                wait(pe, qk_copied, T.n - CORE0)
                tokens = slice(2 * P * T.pair, 2 * P * T.pair + 2 * P)
                for m in range(C):
                    parts = [(w, x, c) for w, x in ((w_hi, x_hi), (w_hi, x_lo), (w_lo, x_hi)) for c in range(C)]
                    for j, (w, x, c) in enumerate(parts):
                        last = mm(bank[5][:, m * D:(m + 1) * D], w[:, which, T.weights, c, m * P:(m + 1) * P],
                                  x[:, c, tokens], start=(j == 0), stop=(j == len(parts) - 1))
                last.then_inc(qk_made, 1)

            def v(T):
                if T.t == 0:
                    pe.wait_ge(ld_wv[T.weights], T.loads())
                wait(pe, o_copied, T.n)
                wait(pe, v_copied, T.n - CORE0)
                w = wv[:, T.weights].rearrange("p c (h j d) -> p c h j d", h=HP, j=2)
                for b in range(2):
                    for h2 in range(2):
                        for c in range(C):
                            last = mm(bank[4][64 * h2:64 * h2 + 64, b * P:(b + 1) * P],
                                      xnT[:, c, T.t * P + 64 * b:T.t * P + 64 * b + 64], w[:, c, :, h2, :],
                                      start=(c == 0), stop=(c == C - 1))
                last.then_inc(v_made, 1)

            def scores3(T):
                first = P * T.two
                core_scores(T, lambda c, b: qT[:, T.pair, c, first + 64 * b:first + 64 * b + 64],
                            qk_copied, T.n + (1 - CORE0 - T.two))

            def heads3(T, later_v):
                core_heads(T, v_copied, later_v)

            def y3(T):
                pe.wait_ge(o_lo_made, T.n - CORE0 + 1)
                if T.i is None and T.c in (0, 2):
                    pe.wait_ge(gT_copied, T.c // 2 + 1)
                if T.t == 0:
                    pe.wait_ge(w_lo_made, T.of_expert(3))
                first = T.i is None and T.c in (0, 2)
                for o, w in ((O_hi, w_hi), (O_lo, w_hi), (O_hi, w_lo)):
                    for c in range(C):
                        last = mm(bank[6 + T.t // 2][:, D * (T.t % 2):D * (T.t % 2) + D], o[:, T.t, c, :],
                                  w[:, 2, T.weights, c, :], start=first, stop=False, skip_group_check=True)
                        first = False
                last.then_inc(y_made, 1)

            def step(k, i=None, bounds=(0, LAST)):
                lo, hi = bounds

                def there(s):
                    return i is not None or lo <= s < hi

                if there(k):
                    scores3(Tile(k, i, CORE0))
                if there(k - 2):
                    before = Tile(k - 1, i, CORE0).n - CORE0
                    heads3(Tile(k - 2, i, CORE0), min(before, LAST) if i is None else before)
                if there(k + 2):
                    qk(Tile(k + 2, i, CORE0))
                if there(k - 1):
                    v(Tile(k - 1, i, CORE0))
                if there(k - 3):
                    y3(Tile(k - 3, i, CORE0))
                if there(k - 1):
                    core_transposes(Tile(k - 1, i, CORE0))

            transpose_xn1(0)
            transpose_xn1(1)
            project1(0)
            project1(1)
            match(0)
            match(1)
            mem_transposes(0)
            keep_warm(1, bank[2], ident, some)
            kv1(0)
            match(2)
            mem_transposes(1)
            scores1(0)
            kv1(1)
            match(3)
            mem_transposes(2)
            scores1(1)
            kv1(2)
            transposes1(0)
            heads1(0)
            scores1(2)
            y1(0)
            mem_transposes(3)
            transposes1(1)
            kv1(3)
            heads1(1)
            y1(1)
            scores1(3)
            transposes1(2)
            transpose_xn2(0)
            heads1(2)
            project(0)
            y1(2)
            project(1)
            project(2)
            transposes1(3)
            project(3)
            heads1(3)
            project(4)
            y1(3)
            project(5)
            project(6)
            project(7)
            project(8)
            project(9)
            project(10)
            project(11)
            transpose_xn2(1)
            scores2(0)
            project(13)
            scores2(1)
            project(12)
            project(15)
            project(14)
            project(17)
            project(16)
            transposes2(0)
            project(19)
            project(18)
            project(21)
            project(20)
            project(23)
            project(22)
            transposes2(1)
            heads2(0, 0)
            scores2(2)
            heads2(0, 1)
            scores2(3)
            heads2(1, 0)
            y2(0)
            heads2(1, 1)
            y2(1)
            transposes2(2)
            heads2(2, 0)
            transposes2(3)
            heads2(2, 1)
            transpose_xn3(0)
            heads2(3, 0)
            y2(2)
            heads2(3, 1)
            router_hidden(0)
            qk(tile(0))
            y2(3)
            router_transposes(0)
            v(tile(0))
            router_logits(0)
            qk(tile(1))
            transpose_xn3(1)
            scores3(tile(0))
            router_hidden(1)
            qk(tile(2))
            gate_transposes(0)
            qk(tile(3))
            scores3(tile(1))
            router_transposes(1)
            core_transposes(tile(0))
            router_logits(1)
            step(2)
            step(3)
            gate_transposes(1)
            for k in range(4, 6):
                step(k)
            with pe.Fori(0, LOOPS) as i:
                for k in range(6, 14):
                    step(k, i)
            for k in range(6 + 8 * LOOPS, LAST):
                step(k)
            heads3(tile(LAST - 2), LAST - 1)
            pe.wait_ge(ld["ob"], 16)
            for t in range(NT):
                mm(bank[6 + t // 2][:, D * (t % 2):D * (t % 2) + D], gatesT[:, t * P:(t + 1) * P], ob[:, :],
                   start=False, stop=False, skip_group_check=True)
            v(tile(LAST - 1))
            core_transposes(tile(LAST - 1))
            y3(tile(LAST - 3))
            y3(tile(LAST - 2))
            heads3(tile(LAST - 1), LAST)
            y3(tile(LAST - 1))

        @block.scalar
        def _(act):
            def copy(dst, src):
                return nc.scalar.activation(dst, src, ACT.Copy)

            def act_kblk(T, k_sem, k_count, shared):
                act.wait_ge(k_sem, k_count)
                wait(act, s_made, T.count(2, -2))
                for h in range(8 - ACT_HEADS, 8):
                    last = nc.scalar.activation(kblk[:, T.two, :, :, h, :], k_of(T, shared), ACT.Copy,
                                                scale=head_mask[:, h:h + 1])
                last.then_inc(kblk_act, 1)

            def core_exp(T):
                for c in range(2):
                    act.wait_ge(sub_done, T.count(2, c + 1))
                    part = E[:, T.two, 8 * c:8 * c + 8].rearrange("p h k -> p (h k)")
                    nc.scalar.activation(part, part, ACT.Exp).then_inc(exp_done, 1)

            def core_copy_pT(T):
                wait(act, o_made, T.count(1, -1))
                for half in range(2):
                    act.wait_ge(pT_made, T.count(2, half + 1))
                    copy(PT[:, T.two, 4 * half:4 * half + 4].rearrange("p h q -> p (h q)"),
                         bank[2 + half][:, :]).then_inc(pT_copied, 1)

            def core_copy_o(T):
                wait(act, y_made, T.count(1, -3))
                act.wait_ge(o_made, T.count(1, 1))
                copy(OT[:, T.t].rearrange("p c q -> p (c q)"), bank[4][:, 0:C * P]).then_inc(o_copied, 1)

            def copy_xT(norm, pair, source):
                act.wait_ge(xT_made, 2 * norm + pair + 1)
                copy(xnT[:, :, 2 * P * pair:2 * P * pair + 2 * P].rearrange("p c (t q) -> p c t q", t=2),
                     source[:, :].rearrange("p (t c q) -> p c t q", t=2, c=C)).then_inc(xT_copied, 1)

            def copy_q1(pair):
                act.wait_ge(q1_made, pair + 1)
                copy(q1T[:, :, D * pair:D * pair + D], bank[4 + pair][:, :].rearrange("p (m q) -> p m q", m=C))\
                  .then_inc(q1_copied, 1)

            def copy_memT(t):
                act.wait_ge(memT_made, t + 1)
                copy(memT[:, t % 2].rearrange("p c q -> p (c q)"), bank[KV_BANK[t]][:, 0:C * P]).then_inc(memT_copied, 1)

            def copy_k1(t):
                act.wait_ge(kv1_made, t + 1)
                wait(act, kblk_dve, t - 1)
                copy(k1T[:, t % 2, :], bank[KV_BANK[t]][:, 256:384]).then_inc(k1_copied, 1)

            def kblk1(t):
                act_kblk(Tile(t), k1_copied, t + 1, True)

            def copy_projected(n):
                act.wait_ge(p2_even, n // 2 + 1)
                copied(n, bank[5], copy, masked).then_inc(p2_act, 1)

            def masked(dst, src, mask):
                return nc.scalar.activation(dst, src, ACT.Copy, scale=mask)

            def exp2(t):
                for half in range(2):
                    act.wait_ge(s2_sub, 2 * t + half + 1)
                    part = E[:, t % 2, 8 * half:8 * half + 8].rearrange("p h k -> p (h k)")
                    nc.scalar.activation(part, part, ACT.Exp).then_inc(s2_exp, 1)

            def copy_pT2(t):
                wait(act, o2_made, 2 * (t - 1))
                for half in range(2):
                    act.wait_ge(pT2_made, 2 * t + half + 1)
                    copy(PT[:, t % 2, 4 * half:4 * half + 4].rearrange("p h q -> p (h q)"),
                         bank[2 + half][:, :]).then_inc(pT2_copied, 1)

            def copy_o2(t, half):
                wait(act, y2_made, t - 1)
                act.wait_ge(o2_made, 2 * t + half + 1)
                copy(O2T[0:64, t % 2, 4 * half:4 * half + 4].rearrange("p h q -> p (h q)"),
                     bank[4][0:64, :]).then_inc(o2_act, 1)

            def tile(k):
                return Tile(k, None, CORE0)

            def copy_x_hi(pair):
                tokens = slice(2 * P * pair, 2 * P * pair + 2 * P)
                copy(x_hi[:, :, tokens].rearrange("p c (t q) -> p c t q", t=2),
                     bank[6 + pair][:, :].rearrange("p (t c q) -> p c t q", t=2, c=C)).then_inc(x_hi_made, 1)

            def router_relu(pair):
                act.wait_ge(hT_made, pair + 1)
                nc.scalar.activation(hidT[:, D * pair:D * pair + D], bank[6 + pair][:, 0:D], ACT.Relu).then_inc(hT_copied, 1)

            def router_exp(pair):
                act.wait_ge(r_exp_in, pair + 1)
                part = prob[:, 2 * pair:2 * pair + 2, :]
                nc.scalar.activation(part, part, ACT.Exp).then_inc(r_exp, 1)

            def copy_gates(pair):
                act.wait_ge(gT_made, pair + 1)
                copy(gatesT[:, D * pair:D * pair + D], bank[6 + pair][0:NE, 0:D]).then_inc(gT_copied, 1)

            def copy_qk(T):
                which = T.c % 2
                act.wait_ge(qk_made, T.n - CORE0 + 1)
                if which == 0:
                    wait(act, s_made, T.count(2, -4))
                else:
                    wait(act, kblk_dve, T.count(1, -3))
                for c in range(C):
                    j = 2 * C * D + which * C + c
                    last = nc.scalar.activation((qT, kT)[which][:, T.pair, c, :], bank[5][:, c * D:(c + 1) * D],
                                                ACT.Identity, bias=wqk[:, T.weights, j:j + 1])
                last.then_inc(qk_copied, 1)

            def kblk3(T):
                act_kblk(T, qk_copied, T.n + (2 - CORE0 - T.two), False)

            def high_part(T, which):
                if which != 1:
                    act.wait_ge((ld_wqk, None, ld_wo)[which][T.weights], T.loads())
                if T.i is None and T.c < 8:
                    act.wait_ge(s2_made, 2 * NT)
                elif which == 2:
                    act.wait_ge(y_made, T.n - 4)
                else:
                    act.wait_ge(qk_made, T.n - CORE0 - 4)
                copy(w_hi[:, which, T.weights], w_of(which, T.weights)).then_inc(w_hi_made, 1)

            def copy_o3(T):
                wait(act, y_made, T.count(1, -3))
                act.wait_ge(o_made, T.count(1, 1))
                source = bank[4][:, 0:C * P]
                copy(OT[:, T.t].rearrange("p c q -> p (c q)"), source)
                copy(O_hi[:, T.t].rearrange("p c q -> p (c q)"), source).then_inc(o_copied, 1)

            def step(k, i=None):
                def there(s):
                    return i is not None or 0 <= s < LAST

                if there(k - 2):
                    core_copy_pT(Tile(k - 2, i, CORE0))
                if k % 4 > 0 and there(k - k % 4 + 4):
                    high_part(Tile(k - k % 4 + 4, i, CORE0), k % 4 - 1)
                if there(k - 2):
                    copy_o3(Tile(k - 2, i, CORE0))
                if there(k + 2):
                    copy_qk(Tile(k + 2, i, CORE0))
                if there(k + 1):
                    kblk3(Tile(k + 1, i, CORE0))
                if there(k):
                    core_exp(Tile(k, i, CORE0))

            copy_xT(0, 0, bank[0])
            copy_xT(0, 1, bank[1])
            copy_q1(0)
            copy_q1(1)
            copy_memT(0)
            copy_k1(0)
            kblk1(0)
            copy_memT(1)
            copy_k1(1)
            kblk1(1)
            core_exp(Tile(0))
            copy_memT(2)
            copy_k1(2)
            kblk1(2)
            core_copy_pT(Tile(0))
            core_exp(Tile(1))
            core_copy_o(Tile(0))
            copy_memT(3)
            core_copy_pT(Tile(1))
            copy_k1(3)
            core_exp(Tile(2))
            core_copy_o(Tile(1))
            kblk1(3)
            core_copy_pT(Tile(2))
            copy_xT(1, 0, bank[5])
            core_exp(Tile(3))
            core_copy_o(Tile(2))
            copy_projected(0)
            copy_projected(2)
            core_copy_pT(Tile(3))
            core_copy_o(Tile(3))
            copy_projected(4)
            copy_projected(6)
            copy_projected(8)
            copy_projected(10)
            copy_xT(1, 1, bank[5])
            exp2(0)
            copy_projected(12)
            copy_projected(14)
            exp2(1)
            copy_projected(16)
            copy_pT2(0)
            copy_projected(18)
            copy_projected(20)
            copy_projected(22)
            copy_pT2(1)
            copy_o2(0, 0)
            copy_o2(0, 1)
            high_part(tile(0), 0)
            copy_o2(1, 0)
            exp2(2)
            high_part(tile(0), 1)
            high_part(tile(0), 2)
            high_part(tile(4), 0)
            copy_o2(1, 1)
            exp2(3)
            copy_pT2(2)
            copy_o2(2, 0)
            copy_pT2(3)
            copy_o2(2, 1)
            copy_xT(2, 0, bank[6])
            copy_x_hi(0)
            copy_o2(3, 0)
            copy_o2(3, 1)
            copy_qk(tile(0))
            router_relu(0)
            copy_qk(tile(1))
            router_exp(0)
            kblk3(tile(0))
            copy_xT(2, 1, bank[7])
            kblk3(tile(1))
            copy_x_hi(1)
            copy_qk(tile(2))
            copy_gates(0)
            core_exp(tile(0))
            copy_qk(tile(3))
            kblk3(tile(2))
            router_relu(1)
            core_exp(tile(1))
            router_exp(1)
            step(2)
            step(3)
            copy_gates(1)
            for k in range(4, 6):
                step(k)
            with act.Fori(0, LOOPS) as i:
                for k in range(6, 14):
                    step(k, i)
            for k in range(6 + 8 * LOOPS, LAST + 2):
                step(k)

        @block.gpsimd
        def _(pool):
            nc.gpsimd.memset(vblk[:, :, :, :, :], 0.0).then_inc(vblk_zero, 1)

            def root(group):
                ts = NORM_GROUPS[group]
                sl = slice(ts[0], ts[-1] + 1)
                pool.wait_ge(ln_mom, sum(len(g) for g in NORM_GROUPS[:group + 1]))
                nc.gpsimd.tensor_scalar(rstd[:, sl], moments[:, sl, 1], EPS, None, ALU.add).then_inc(ln_eps, 1)
                pool.wait_ge(ln_eps, group + 1)
                nc.gpsimd.tensor_tensor(rstd[:, sl], rstd[:, sl], minus_half[:, 0:len(ts)], ALU.pow)\
                  .then_inc(ln_rstd, 1)

            def scale(two, r, r_sem, r_count, done):
                pool.wait_ge(r_sem, r_count)
                nc.gpsimd.tensor_tensor(E[:, two], E[:, two], r[:, two, :].unsqueeze(2).to_broadcast([P, H, L]),
                                        ALU.mult).then_inc(done, 1)

            pool.wait_ge(ld["const"], 16)

            def replicate_w1k():
                pool.wait_ge(ld["w1kv"], 16)
                nc.gpsimd.tensor_copy(w1kr[:, :, :, :], w1kv[:, :, 0:16].unsqueeze(2).to_broadcast([P, C, 8, 16]))\
                  .then_inc(w1kr_ready, 1)

            def gather(t):
                pool.wait_ge(rows_ready, t + 1)
                pool.indirect_dma_start(
                    mem[:, t, :], None, A["ctx"],
                    bass.IndirectOffsetOnAxis(ap=rows[:, t:t + 1], axis=0)).then_inc(ld_mem[t], 16)
                nc.gpsimd.memset(asked[:, t:t + 1], 0.0).then_inc(rows_asked, 1)

            def scale1(t):
                scale(t % 2, recip, recip_done, t + 1, p_ready)

            def scale2(t):
                scale(t % 2, recip, s2_recip, t + 1, s2_p)

            def scale3(T):
                scale(T.two, rgate, r_ready, T.n - CORE0 + 1, p_ready)

            def tile(k):
                return Tile(k, None, CORE0)

            def low_part(T, which):
                pool.wait_ge(w_hi_made, T.of_expert(which + 1))
                nc.gpsimd.tensor_tensor(w_lo[:, which, T.weights], w_of(which, T.weights),
                                        w_hi[:, which, T.weights].bitcast(F32), ALU.subtract).then_inc(w_lo_made, 1)

            def o_low_part(T):
                pool.wait_ge(o_copied, T.count(1, 1))
                nc.gpsimd.tensor_tensor(O_lo[:, T.t], OT[:, T.t], O_hi[:, T.t].bitcast(F32), ALU.subtract)\
                  .then_inc(o_lo_made, 1)

            def x_low_part(pair):
                pool.wait_ge(x_hi_made, pair + 1)
                tokens = slice(2 * P * pair, 2 * P * pair + 2 * P)
                nc.gpsimd.tensor_tensor(x_lo[:, :, tokens], xnT[:, :, tokens], x_hi[:, :, tokens].bitcast(F32),
                                        ALU.subtract).then_inc(x_lo_made, 1)

            def step(k, i=None):
                def there(s):
                    return i is not None or 0 <= s < LAST

                if there(k - 1):
                    scale3(Tile(k - 1, i, CORE0))
                if there(k - 2):
                    o_low_part(Tile(k - 2, i, CORE0))
                if k % 4 > 0 and there(k - k % 4 + 4):
                    low_part(Tile(k - k % 4 + 4, i, CORE0), k % 4 - 1)

            root(STAGE_NORM[0][0])
            root(STAGE_NORM[0][1])
            replicate_w1k()
            gather(0)
            gather(1)
            gather(2)
            scale1(0)
            gather(3)
            scale1(1)
            scale1(2)
            root(STAGE_NORM[1][0])
            scale1(3)
            root(STAGE_NORM[1][1])
            scale2(0)
            scale2(1)
            low_part(tile(0), 0)
            low_part(tile(0), 1)
            low_part(tile(0), 2)
            low_part(tile(4), 0)
            scale2(2)
            scale2(3)
            root(STAGE_NORM[2][0])
            x_low_part(0)
            root(ROUTER_NORM[0])
            root(STAGE_NORM[2][1])
            x_low_part(1)
            root(ROUTER_NORM[1])
            scale3(tile(0))
            for k in range(2, 6):
                step(k)
            with pool.Fori(0, LOOPS) as i:
                for k in range(6, 14):
                    step(k, i)
            for k in range(6 + 8 * LOOPS, LAST + 2):
                step(k)

        @block.vector
        def _(dve):
            ve = nc.vector

            def bc(ap, n):
                return ap.unsqueeze(2).to_broadcast([P, ap.shape[1], n])

            def norm_moments(group, src):
                ts, before = NORM_GROUPS[group], sum(len(g) for g in NORM_GROUPS[:group])
                for t in ts:
                    ve.bn_stats(stats[:, t], src(t)).then_inc(ln_stat, 1)
                for j, t in enumerate(ts):
                    dve.wait_ge(ln_stat, before + j + 1)
                    ve.bn_aggr(moments[:, t], stats[:, t]).then_inc(ln_mom, 1)

            def norm_apply(group, src, dst, done):
                dve.wait_ge(ln_rstd, group + 1)
                for t in NORM_GROUPS[group]:
                    ve.tensor_scalar(dst(t), src(t), moments[:, t, 0:1], rstd[:, t:t + 1],
                                     ALU.subtract, ALU.mult).then_inc(done, 1)

            def core_kblk(T, k_sem, k_count, shared):
                dve.wait_ge(k_sem, k_count)
                wait(dve, s_made, T.count(2, -2))
                for h in range(8 - ACT_HEADS):
                    last = ve.tensor_scalar(kblk[:, T.two, :, :, h, :], k_of(T, shared), head_mask[:, h:h + 1], None,
                                            ALU.mult)
                last.then_inc(kblk_dve, 1)

            def core_max(T, c):
                dve.wait_ge(s_made, T.count(2, c + 1))
                ve.tensor_reduce(mx[:, T.two, 8 * c:8 * c + 8], bank[c][:, :].rearrange("p (h k) -> p h k", h=8),
                                 AX.X, ALU.max).then_inc(max_done, 1)

            def core_less_max(T):
                wait(dve, pT_made, T.count(2, -2))
                for c in range(2):
                    dve.wait_ge(max_done, T.count(2, c + 1))
                    ve.tensor_tensor(E[:, T.two, 8 * c:8 * c + 8], bank[c][:, :].rearrange("p (h k) -> p h k", h=8),
                                     bc(mx[:, T.two, 8 * c:8 * c + 8], L), ALU.subtract).then_inc(sub_done, 1)

            def core_softmax(T):
                core_max(T, 0)
                core_max(T, 1)
                core_less_max(T)

            def core_sum(T):
                wait(dve, p_ready, T.count(1, -1))
                for c in range(2):
                    dve.wait_ge(exp_done, T.count(2, c + 1))
                    ve.tensor_reduce(ssum[:, T.two, 8 * c:8 * c + 8], E[:, T.two, 8 * c:8 * c + 8], AX.X, ALU.add)\
                      .then_inc(sum_done, 1)

            def core_recip(T):
                dve.wait_ge(sum_done, T.count(2, 2))
                ve.reciprocal(recip[:, T.two], ssum[:, T.two]).then_inc(recip_done, 1)

            def core_gate(T):
                dve.wait_ge(recip_done, T.count(1, 1))
                e = T.expert
                gate = gates[:, T.t, e:e + 1] if isinstance(e, int) else gates[:, T.t, bass.ds(e, 1)]
                ve.tensor_scalar(rgate[:, T.two], recip[:, T.two], gate, None, ALU.mult).then_inc(r_ready, 1)

            def sum1(t):
                core_sum(Tile(t))
                core_recip(Tile(t))

            def sum3(T):
                core_sum(T)
                core_recip(T)
                core_gate(T)

            def moments1(pair):
                dve.wait_ge(ld_x[pair], 16)
                norm_moments(STAGE_NORM[0][pair], lambda t: xres[:, t])

            def norm1(pair):
                norm_apply(STAGE_NORM[0][pair], lambda t: xres[:, t], lambda t: xn[:, t], ln_done)

            def search(t):
                dve.wait_ge(match_made, t + 1)
                whole = pair_of_banks[MATCH_PAIR[t]][:, :]
                ve.max(top8[:, t], whole).then_inc(match_max, 1)
                dve.wait_ge(match_max, t + 1)
                ve.max_index(top8i[:, t], top8[:, t], whole).then_inc(match_read, 1)
                dve.wait_ge(match_read, t + 1)
                if t == 0:
                    dve.wait_ge(ld["row_base"], 16)
                    dve.wait_ge(ld["const"], 16)
                    dve.wait_ge(vblk_zero, 1)
                ve.tensor_tensor(rows[:, t:t + 1], top8i[:, t, 0:1], row_base[:, t:t + 1], ALU.add)\
                  .then_inc(rows_ready, 1)

            def copy_v1(t):
                dve.wait_ge(k1_copied, t + 1)
                wait(dve, o_made, t - 1)
                for h2 in range(2):
                    r = slice(64 * h2, 64 * h2 + 64)
                    for b in range(2):
                        last = ve.tensor_copy(
                            vblk[r, t % 2, b, :, 16 * h2:16 * h2 + 16],
                            bank[KV_BANK[t]][r, 384 + 16 * b:400 + 16 * b].unsqueeze(1).to_broadcast([64, HP, 16]))
                last.then_inc(v1_copied, 1)

            def add_y(stage, pair, made):
                dve.wait_ge(made, 2 * pair + 2)
                for t in (2 * pair, 2 * pair + 1):
                    ve.tensor_tensor(xres[:, t], bank[6 + pair][:, D * (t % 2):D * (t % 2) + D], xres[:, t], ALU.add)\
                      .then_inc(x_added, 1)
                dve.wait_ge(x_added, NT * stage + 2 * pair + 2)
                norm_moments(STAGE_NORM[stage + 1][pair], lambda t: xres[:, t])

            def norm_y(stage, pair):
                norm_apply(STAGE_NORM[stage + 1][pair], lambda t: xres[:, t], lambda t: xn[:, t], ln_done)

            def kblk1(t):
                core_kblk(Tile(t), k1_copied, t + 1, True)

            def copy_projected(n):
                dve.wait_ge(p2_odd, n // 2 + 1)
                copied(n, bank[6 + n // PROJECTED], ve.tensor_copy, masked).then_inc(p2_dve, 1)

            def masked(dst, src, mask):
                return ve.tensor_scalar(dst, src, mask, None, ALU.mult)

            def mask2(t):
                wait(dve, pT2_made, 2 * (t - 1))
                for half in range(2):
                    hs = slice(8 * half, 8 * half + 8)
                    dve.wait_ge(s2_made, 2 * t + half + 1)
                    ve.tensor_tensor(E[:, t % 2, hs], bank[half][:, :].rearrange("p (h k) -> p h k", h=8),
                                     causal.unsqueeze(1).to_broadcast([P, 8, L]), ALU.add).then_inc(s2_masked, 1)

            def softmax2(t):
                for half in range(2):
                    hs = slice(8 * half, 8 * half + 8)
                    dve.wait_ge(s2_masked, 2 * t + half + 1)
                    ve.tensor_reduce(mx[:, t % 2, hs], E[:, t % 2, hs], AX.X, ALU.max).then_inc(s2_max, 1)
                for half in range(2):
                    hs = slice(8 * half, 8 * half + 8)
                    dve.wait_ge(s2_max, 2 * t + half + 1)
                    ve.tensor_tensor(E[:, t % 2, hs], E[:, t % 2, hs], bc(mx[:, t % 2, hs], L), ALU.subtract)\
                      .then_inc(s2_sub, 1)

            def sum2(t):
                wait(dve, s2_p, t - 1)
                for half in range(2):
                    hs = slice(8 * half, 8 * half + 8)
                    dve.wait_ge(s2_exp, 2 * t + half + 1)
                    ve.tensor_reduce(ssum[:, t % 2, hs], E[:, t % 2, hs], AX.X, ALU.add).then_inc(s2_sum, 1)
                dve.wait_ge(s2_sum, 2 * t + 2)
                ve.reciprocal(recip[:, t % 2], ssum[:, t % 2]).then_inc(s2_recip, 1)

            def copy_o2(t, half):
                wait(dve, y2_made, t - 1)
                dve.wait_ge(o2_made, 2 * t + half + 1)
                ve.tensor_copy(O2T[64:128, t % 2, 4 * half:4 * half + 4].rearrange("p h q -> p (h q)"),
                               bank[4][64:128, :]).then_inc(o2_dve, 1)

            links = [0]

            def link(ins):
                links[0] += 1
                ins.then_inc(r_chain, 1)
                dve.wait_ge(r_chain, links[0])

            def tiles_of(pair):
                return slice(2 * pair, 2 * pair + 2)

            def router_bias(pair):
                if pair == 0:
                    dve.wait_ge(ld["router"], 96)
                dve.wait_ge(h_made, pair + 1)
                link(ve.tensor_tensor(hid[:, tiles_of(pair), :], bank[6 + pair][:, 0:D].rearrange("p (t j) -> p t j", t=2),
                                      rb1[:, :].unsqueeze(1).to_broadcast([P, 2, P]), ALU.add))
                norm_moments(ROUTER_NORM[pair], lambda t: hid[:, t])

            def router_norm(pair):
                part = hid[:, tiles_of(pair), :]
                norm_apply(ROUTER_NORM[pair], lambda t: hid[:, t], lambda t: hid[:, t], hid_normed)
                dve.wait_ge(hid_normed, 2 * pair + 2)
                link(ve.tensor_tensor(part, part, lng[:, :].unsqueeze(1).to_broadcast([P, 2, P]), ALU.mult))
                ve.tensor_tensor(part, part, lnb[:, :].unsqueeze(1).to_broadcast([P, 2, P]), ALU.add).then_inc(h_ready, 1)

            def router_max(pair):
                ts = tiles_of(pair)
                dve.wait_ge(l_made, pair + 1)
                link(ve.tensor_tensor(logit[:, ts, :], bank[6 + pair][:, D:D + 2 * NE].rearrange("p (t e) -> p t e", t=2),
                                      rb2[:, :].unsqueeze(1).to_broadcast([P, 2, NE]), ALU.add))
                link(ve.tensor_reduce(rtmp[:, 0, ts], logit[:, ts, :], AX.X, ALU.max))
                ve.tensor_tensor(prob[:, ts, :], logit[:, ts, :], bc(rtmp[:, 0, ts], NE), ALU.subtract)\
                  .then_inc(r_exp_in, 1)

            def router_gates(pair):
                ts = tiles_of(pair)
                both = (2 * pair, 2 * pair + 1)
                dve.wait_ge(r_exp, pair + 1)
                link(ve.tensor_reduce(rtmp[:, 1, ts], prob[:, ts, :], AX.X, ALU.add))
                link(ve.reciprocal(rtmp[:, 2, ts], rtmp[:, 1, ts]))
                link(ve.tensor_tensor(prob[:, ts, :], prob[:, ts, :], bc(rtmp[:, 2, ts], NE), ALU.mult))
                for t in both:
                    last = ve.max(ptop[:, t], prob[:, t])
                link(last)
                for t in both:
                    ve.max_index(itop[:, t], ptop[:, t], prob[:, t])
                link(ve.tensor_reduce(rtmp[:, 3, ts], ptop[:, ts, 0:2], AX.X, ALU.add))
                ve.tensor_copy(itopf[:, ts, :], itop[:, ts, :])
                link(ve.reciprocal(rtmp[:, 1, ts], rtmp[:, 3, ts]))

                def by_rank(top):
                    return top[:, ts, 0:2].rearrange("p t r -> p r t").unsqueeze(3).to_broadcast([P, 2, 2, NE])

                link(ve.tensor_tensor(pick[:, :, ts], iota.unsqueeze(1).unsqueeze(1).to_broadcast([P, 2, 2, NE]),
                                      by_rank(itopf), ALU.is_equal))
                link(ve.tensor_tensor(pick[:, :, ts], pick[:, :, ts], by_rank(ptop), ALU.mult))
                link(ve.tensor_tensor(pick[:, 0, ts], pick[:, 0, ts], pick[:, 1, ts], ALU.add))
                ve.tensor_tensor(gates[:, ts, :], pick[:, 0, ts], bc(rtmp[:, 1, ts], NE), ALU.mult).then_inc(gates_ready, 1)
                dve.wait_ge(gates_ready, pair + 1)

            def tile(k):
                return Tile(k, None, CORE0)

            def kblk3(T):
                core_kblk(T, qk_copied, T.n + (2 - CORE0 - T.two), False)

            def copy_v(T):
                dve.wait_ge(v_made, T.n - CORE0 + 1)
                wait(dve, o_made, T.count(1, -1))
                if T.t == 0:
                    dve.wait_ge(ld_vb[T.weights], T.loads())
                bias = vb[:, T.weights, :].rearrange("p (h j d) -> p h j d", h=HP, j=2)
                for h2 in range(2):
                    r = slice(64 * h2, 64 * h2 + 64)
                    last = ve.tensor_tensor(
                        vblk[r, T.two, :, :, 16 * h2:16 * h2 + 16],
                        bank[4][r, 0:2 * P].rearrange("p (b h d) -> p b h d", b=2, h=HP),
                        bias[r, :, h2, :].unsqueeze(1).to_broadcast([64, 2, HP, 16]), ALU.add)
                last.then_inc(v_copied, 1)

            def step(k, i=None):
                def there(s):
                    return i is not None or 0 <= s < LAST

                if there(k - 1):
                    core_sum(Tile(k - 1, i, CORE0))
                if there(k):
                    core_max(Tile(k, i, CORE0), 0)
                if there(k - 1):
                    core_recip(Tile(k - 1, i, CORE0))
                if there(k):
                    core_max(Tile(k, i, CORE0), 1)
                if there(k - 1):
                    core_gate(Tile(k - 1, i, CORE0))
                if there(k):
                    core_less_max(Tile(k, i, CORE0))
                if there(k + 1):
                    kblk3(Tile(k + 1, i, CORE0))
                if there(k - 1):
                    copy_v(Tile(k - 1, i, CORE0))

            moments1(0)
            moments1(1)
            norm1(0)
            norm1(1)
            search(0)
            search(1)
            copy_v1(0)
            kblk1(0)
            search(2)
            core_softmax(Tile(0))
            copy_v1(1)
            kblk1(1)
            sum1(0)
            search(3)
            core_softmax(Tile(1))
            kblk1(2)
            copy_v1(2)
            sum1(1)
            core_softmax(Tile(2))
            kblk1(3)
            sum1(2)
            add_y(0, 0, y_made)
            copy_v1(3)
            norm_y(0, 0)
            core_softmax(Tile(3))
            sum1(3)
            copy_projected(1)
            copy_projected(3)
            add_y(0, 1, y_made)
            copy_projected(5)
            norm_y(0, 1)
            copy_projected(7)
            copy_projected(9)
            copy_projected(11)
            mask2(0)
            softmax2(0)
            copy_projected(13)
            mask2(1)
            sum2(0)
            copy_projected(15)
            softmax2(1)
            copy_projected(17)
            sum2(1)
            copy_projected(19)
            copy_projected(21)
            copy_projected(23)
            copy_o2(0, 0)
            mask2(2)
            copy_o2(0, 1)
            softmax2(2)
            mask2(3)
            copy_o2(1, 0)
            softmax2(3)
            copy_o2(1, 1)
            sum2(2)
            sum2(3)
            add_y(1, 0, y2_made)
            copy_o2(2, 0)
            norm_y(1, 0)
            copy_o2(2, 1)
            copy_o2(3, 0)
            copy_o2(3, 1)
            router_bias(0)
            router_norm(0)
            add_y(1, 1, y2_made)
            copy_v(tile(0))
            router_max(0)
            norm_y(1, 1)
            kblk3(tile(0))
            router_gates(0)
            kblk3(tile(1))
            core_softmax(tile(0))
            router_bias(1)
            sum3(tile(0))
            router_norm(1)
            kblk3(tile(2))
            core_softmax(tile(1))
            router_max(1)
            step(2)
            router_gates(1)
            for k in range(3, 6):
                step(k)
            with dve.Fori(0, LOOPS) as i:
                for k in range(6, 14):
                    step(k, i)
            for k in range(6 + 8 * LOOPS, LAST + 2):
                step(k)
            for pair in range(2):
                dve.wait_ge(y_made, CORE0 + LAST - 2 + 2 * pair)
                for t in (2 * pair, 2 * pair + 1):
                    ve.tensor_tensor(final[:, t], bank[6 + pair][:, D * (t % 2):D * (t % 2) + D], xres[:, t], ALU.add)\
                      .then_inc(final_ready, 1)


def kernel(**inputs):
    import numpy as np
    import concourse.bacc as bacc
    from concourse.bass_utils import run_bass_kernel_spmd

    def halves(w):
        n, k = w.shape
        return np.ascontiguousarray(w.T.reshape(k // P, P, n).transpose(1, 0, 2))

    g = {k: np.asarray(v) for k, v in inputs.items()}
    x, ctx = g["x"], g["ctx_1024"]
    b, l, d = x.shape
    m = ctx.shape[1]
    ne = g["L0_ffn_qW"].shape[0]
    a = {
        "x": np.ascontiguousarray(x.reshape(b * l, d)),
        "ctx": np.ascontiguousarray(ctx.reshape(b * m, d)),
        "ctxT": np.ascontiguousarray(ctx.transpose(0, 2, 1).reshape(b, d // P, P, m).transpose(0, 2, 1, 3)),
        "w1q": halves(g["L0_xattn_Wq"]),
        "w1kv": halves(g["L0_xattn_Wkv"]),
        "w1c": halves(g["L0_xattn_Wc"]),
        "w2q": halves(g["L0_attn_wq"]),
        "w2k": halves(g["L0_attn_wk"]),
        "w2v": halves(g["L0_attn_wv"]),
        "w2o": halves(g["L0_attn_wo"]),
        "rw1": halves(g["L0_ffn_rW1"]),
        "rw2": np.ascontiguousarray(g["L0_ffn_rW2"].T),
        "rb1": np.ascontiguousarray(g["L0_ffn_rb1"].reshape(1, -1)),
        "ln_g": np.ascontiguousarray(g["L0_ffn_ln_g"].reshape(1, -1)),
        "ln_b": np.ascontiguousarray(g["L0_ffn_ln_b"].reshape(1, -1)),
        "rb2": np.ascontiguousarray(g["L0_ffn_rb2"].reshape(1, -1)),
        "ob": np.ascontiguousarray(g["L0_ffn_ob"]),
        "vb": np.ascontiguousarray(g["L0_ffn_vb"]),
    }
    packs = []
    for e in range(ne):
        parts = [halves(g[f"L0_ffn_{n}W"][e]).reshape(P, -1) for n in "qk"]
        parts += [g[f"L0_ffn_{n}b"][e].reshape(d // P, P).T for n in "qk"]
        packs.append(np.concatenate(parts, axis=1))
    a["w_qk"] = np.ascontiguousarray(np.stack(packs))
    a["w_v"] = np.ascontiguousarray(np.stack([halves(g["L0_ffn_vW"][e]) for e in range(ne)]))
    a["w_o"] = np.ascontiguousarray(np.stack([halves(g["L0_ffn_oW"][e]) for e in range(ne)]))

    row = np.arange(P)[:, None]
    const = np.concatenate([
        np.eye(P),
        0.25 * (row // 16 == np.arange(8)),
        0.125 * (row // 64 == np.arange(2)),
        np.where(np.arange(l) <= row % l, 0.0, -3e38),
        np.broadcast_to(np.arange(8), (P, 8)),
        np.full((P, 4), -0.5),
    ], axis=1).astype(np.float32)
    a["const"] = np.ascontiguousarray(const)
    a["row_base"] = np.ascontiguousarray(((2 * np.arange(4)[None, :] + row // l) * m).astype(np.uint32))

    nc = bacc.Bacc("TRN2", target_bir_lowering=False, num_devices=1)
    aps, arrays = {}, {}
    for name, v in a.items():
        arrays[f"in_{name}"] = v
        aps[name] = nc.dram_tensor(f"in_{name}", v.shape, mybir.dt.from_np(v.dtype), kind="ExternalInput").ap()
    aps["out"] = nc.dram_tensor("out_0", (b * l, d), F32, kind="ExternalOutput").ap()
    build(nc, aps)
    r = run_bass_kernel_spmd(nc, [arrays], core_ids=[0])
    return r.results[0]["out_0"].reshape(b, l, d)
```
